# Optimizing a Trainium2 kernel written in Bass

```python
import numpy as np
import jax
import jax.numpy as jnp

def _softmax(x, axis=-1):
    return jax.nn.softmax(x, axis=axis)

def _gelu(x):
    return jax.nn.gelu(x, approximate=True)

def _silu(x):
    return jax.nn.silu(x)

def _sigmoid(x):
    return jax.nn.sigmoid(x)

def _layernorm(x, axis=-1, eps=1e-05):
    m = jnp.mean(x, axis=axis, keepdims=True)
    v = jnp.var(x, axis=axis, keepdims=True)
    return (x - m) / jnp.sqrt(v + eps)

def _scatter_add(tgt, idx, src, axis=0):
    return tgt.at[idx].add(src)

def _segment_sum(src, seg, n):
    return jax.ops.segment_sum(src, seg, n)
kernel_name = 'mk_prb_d1_jaxref_r4_74323e'

def setup_inputs(seed: int=0):
    np.random.seed(seed)
    _w = jnp.asarray

    def _L0_attn_setup():
        import math
        import jax, jax.numpy as jnp
        import numpy as np
        EMBED_DIM = 512
        NUM_HEADS = 16
        HEAD_DIM = EMBED_DIM // NUM_HEADS
        CHUNK = 128
        RMS_EPS = 1e-05

        def _build_slopes(n):

            def pow2(n):
                start = 2.0 ** (-2.0 ** (-(math.log2(n) - 3)))
                return [start * start ** i for i in range(n)]
            if math.log2(n).is_integer():
                s = pow2(n)
            else:
                closest = 2 ** math.floor(math.log2(n))
                s = pow2(closest) + pow2(2 * closest)[0::2][:n - closest]
            return jnp.asarray(s, dtype=jnp.float32)

        def _rotary(x_BTHD, offset=0):
            T, D = (x_BTHD.shape[1], x_BTHD.shape[-1])
            freq = (1.0 / 1024.0) ** jnp.linspace(0.0, 1.0, D // 4, dtype=jnp.float32)
            freq = jnp.concatenate([freq, jnp.zeros(D // 4, dtype=jnp.float32)])
            t = jnp.arange(offset, offset + T, dtype=jnp.float32)
            theta = t[:, None] * freq[None, :]
            cos = jnp.cos(theta)[None, :, None, :]
            sin = jnp.sin(theta)[None, :, None, :]
            x1, x2 = jnp.split(x_BTHD.astype(jnp.float32), 2, axis=-1)
            y1 = x1 * cos + x2 * sin
            y2 = -x1 * sin + x2 * cos
            return jnp.concatenate([y1, y2], axis=-1).astype(x_BTHD.dtype)

        def _lightning_attn(q, k, v, slopes):
            B, H, T, D = q.shape
            C = CHUNK
            NC = T // C
            r = jnp.exp(-slopes)
            i = jnp.arange(C, dtype=jnp.float32)
            q_decay = r[:, None] ** (i[None, :] + 1.0)
            k_decay = r[:, None] ** (C - 1.0 - i[None, :])
            diff = i[:, None] - i[None, :]
            mask = diff >= 0
            dmask = jnp.where(mask[None], r[:, None, None] ** jnp.where(mask, diff, 0.0)[None], 0.0)
            r_C = r ** float(C)

            def reshape_chunks(x):
                return x.reshape(B, H, NC, C, D).transpose(2, 0, 1, 3, 4)
            qc, kc, vc = (reshape_chunks(q), reshape_chunks(k), reshape_chunks(v))

            def step(kv, qkv):
                qi, ki, vi = qkv
                inter = jnp.einsum('bhcd,bhde->bhce', qi * q_decay[None, :, :, None], kv)
                scores = jnp.einsum('bhcd,bhsd->bhcs', qi, ki) * dmask[None]
                intra = jnp.einsum('bhcs,bhse->bhce', scores, vi)
                kv_new = r_C[None, :, None, None] * kv + jnp.einsum('bhcd,bhce->bhde', ki * k_decay[None, :, :, None], vi)
                return (kv_new, inter + intra)
            kv0 = jnp.zeros((B, H, D, D), dtype=q.dtype)
            _, out = jax.lax.scan(step, kv0, (qc, kc, vc))
            return out.transpose(1, 2, 0, 3, 4).reshape(B, H, T, D)

        def _rms_norm(x, w):
            var = jnp.mean(jnp.square(x), axis=-1, keepdims=True)
            return x * jax.lax.rsqrt(var + RMS_EPS) * w
        key = jax.random.key(seed)
        ks = jax.random.split(key, 6)
        sc = 1.0 / math.sqrt(EMBED_DIM)
        return {'x': jax.random.normal(ks[0], (4, 1024, EMBED_DIM), dtype=jnp.float32), 'Wq': jax.random.normal(ks[1], (EMBED_DIM, EMBED_DIM), dtype=jnp.float32) * sc, 'Wk': jax.random.normal(ks[2], (EMBED_DIM, EMBED_DIM), dtype=jnp.float32) * sc, 'Wv': jax.random.normal(ks[3], (EMBED_DIM, EMBED_DIM), dtype=jnp.float32) * sc, 'Wo': jax.random.normal(ks[4], (EMBED_DIM, EMBED_DIM), dtype=jnp.float32) * sc, 'rms_w': jnp.ones((EMBED_DIM,), dtype=jnp.float32)}
    _L0_attn_in = _L0_attn_setup()

    def _L0_ffn_setup():
        import jax, jax.numpy as jnp
        import numpy as np
        TARGET_SPARSITY = 0.9
        LN_EPS = 1e-05

        def ternary_quant(W):
            scale = jnp.mean(jnp.abs(W))
            q = jnp.clip(jnp.round(W / (scale + 1e-08)), -1.0, 1.0) * scale
            return W + jax.lax.stop_gradient(q - W)

        def layernorm(x, gamma, beta):
            mu = jnp.mean(x, axis=-1, keepdims=True)
            var = jnp.var(x, axis=-1, keepdims=True)
            return (x - mu) * jax.lax.rsqrt(var + LN_EPS) * gamma + beta
        key = jax.random.key(seed)
        ks = jax.random.split(key, 3)
        B, S, D, N = (4, 512, 512, 2048)
        x = jax.random.normal(ks[0], (B, S, D), dtype=jnp.float32)
        W_syn = jax.random.normal(ks[1], (N, D), dtype=jnp.float32) * (1.0 / np.sqrt(D))
        b_syn = jnp.zeros((N,), dtype=jnp.float32)
        W_out = jax.random.normal(ks[2], (D, N), dtype=jnp.float32) * (1.0 / np.sqrt(N))
        b_out = jnp.zeros((D,), dtype=jnp.float32)
        gamma = jnp.ones((D,), dtype=jnp.float32)
        beta = jnp.zeros((D,), dtype=jnp.float32)
        return {'x': x, 'W_syn': W_syn, 'b_syn': b_syn, 'W_out': W_out, 'b_out': b_out, 'gamma': gamma, 'beta': beta}
    _L0_ffn_in = _L0_ffn_setup()
    _d = {'L0_attn_x': _L0_attn_in['x'], 'L0_attn_Wq': _L0_attn_in['Wq'], 'L0_attn_Wk': _L0_attn_in['Wk'], 'L0_attn_Wv': _L0_attn_in['Wv'], 'L0_attn_Wo': _L0_attn_in['Wo'], 'L0_attn_rms_w': _L0_attn_in['rms_w'], 'L0_ffn_W_syn': _L0_ffn_in['W_syn'], 'L0_ffn_b_syn': _L0_ffn_in['b_syn'], 'L0_ffn_W_out': _L0_ffn_in['W_out'], 'L0_ffn_b_out': _L0_ffn_in['b_out'], 'L0_ffn_gamma': _L0_ffn_in['gamma'], 'L0_ffn_beta': _L0_ffn_in['beta']}
    _x0 = _d['L0_attn_x']
    _d['L0_attn_x'] = jax.random.normal(jax.random.fold_in(jax.random.key(seed), 1), (4, 1024, 512), dtype=_x0.dtype)
    del _x0
    return _d

def reference(L0_attn_x, L0_attn_Wq, L0_attn_Wk, L0_attn_Wv, L0_attn_Wo, L0_attn_rms_w, L0_ffn_W_syn, L0_ffn_b_syn, L0_ffn_W_out, L0_ffn_b_out, L0_ffn_gamma, L0_ffn_beta):

    def _L0_attn_ref(x, Wq, Wk, Wv, Wo, rms_w):
        import math
        import jax, jax.numpy as jnp
        import numpy as np
        EMBED_DIM = 512
        NUM_HEADS = 16
        HEAD_DIM = EMBED_DIM // NUM_HEADS
        CHUNK = 128
        RMS_EPS = 1e-05

        def _build_slopes(n):

            def pow2(n):
                start = 2.0 ** (-2.0 ** (-(math.log2(n) - 3)))
                return [start * start ** i for i in range(n)]
            if math.log2(n).is_integer():
                s = pow2(n)
            else:
                closest = 2 ** math.floor(math.log2(n))
                s = pow2(closest) + pow2(2 * closest)[0::2][:n - closest]
            return jnp.asarray(s, dtype=jnp.float32)

        def _rotary(x_BTHD, offset=0):
            T, D = (x_BTHD.shape[1], x_BTHD.shape[-1])
            freq = (1.0 / 1024.0) ** jnp.linspace(0.0, 1.0, D // 4, dtype=jnp.float32)
            freq = jnp.concatenate([freq, jnp.zeros(D // 4, dtype=jnp.float32)])
            t = jnp.arange(offset, offset + T, dtype=jnp.float32)
            theta = t[:, None] * freq[None, :]
            cos = jnp.cos(theta)[None, :, None, :]
            sin = jnp.sin(theta)[None, :, None, :]
            x1, x2 = jnp.split(x_BTHD.astype(jnp.float32), 2, axis=-1)
            y1 = x1 * cos + x2 * sin
            y2 = -x1 * sin + x2 * cos
            return jnp.concatenate([y1, y2], axis=-1).astype(x_BTHD.dtype)

        def _lightning_attn(q, k, v, slopes):
            B, H, T, D = q.shape
            C = CHUNK
            NC = T // C
            r = jnp.exp(-slopes)
            i = jnp.arange(C, dtype=jnp.float32)
            q_decay = r[:, None] ** (i[None, :] + 1.0)
            k_decay = r[:, None] ** (C - 1.0 - i[None, :])
            diff = i[:, None] - i[None, :]
            mask = diff >= 0
            dmask = jnp.where(mask[None], r[:, None, None] ** jnp.where(mask, diff, 0.0)[None], 0.0)
            r_C = r ** float(C)

            def reshape_chunks(x):
                return x.reshape(B, H, NC, C, D).transpose(2, 0, 1, 3, 4)
            qc, kc, vc = (reshape_chunks(q), reshape_chunks(k), reshape_chunks(v))

            def step(kv, qkv):
                qi, ki, vi = qkv
                inter = jnp.einsum('bhcd,bhde->bhce', qi * q_decay[None, :, :, None], kv)
                scores = jnp.einsum('bhcd,bhsd->bhcs', qi, ki) * dmask[None]
                intra = jnp.einsum('bhcs,bhse->bhce', scores, vi)
                kv_new = r_C[None, :, None, None] * kv + jnp.einsum('bhcd,bhce->bhde', ki * k_decay[None, :, :, None], vi)
                return (kv_new, inter + intra)
            kv0 = jnp.zeros((B, H, D, D), dtype=q.dtype)
            _, out = jax.lax.scan(step, kv0, (qc, kc, vc))
            return out.transpose(1, 2, 0, 3, 4).reshape(B, H, T, D)

        def _rms_norm(x, w):
            var = jnp.mean(jnp.square(x), axis=-1, keepdims=True)
            return x * jax.lax.rsqrt(var + RMS_EPS) * w
        B, T, E = x.shape
        H, D = (NUM_HEADS, HEAD_DIM)
        q = (x @ Wq).reshape(B, T, H, D)
        k = (x @ Wk).reshape(B, T, H, D)
        v = (x @ Wv).reshape(B, T, H, D)
        q = _rotary(q)
        k = _rotary(k)
        q, k, v = (t.transpose(0, 2, 1, 3) for t in (q, k, v))
        slopes = _build_slopes(H)
        attn = _lightning_attn(q, k, v, slopes)
        attn = attn.transpose(0, 2, 1, 3).reshape(B, T, E)
        attn = _rms_norm(attn, rms_w)
        return attn @ Wo

    def _L0_ffn_ref(x, W_syn, b_syn, W_out, b_out, gamma, beta):
        import jax, jax.numpy as jnp
        import numpy as np
        TARGET_SPARSITY = 0.9
        LN_EPS = 1e-05

        def ternary_quant(W):
            scale = jnp.mean(jnp.abs(W))
            q = jnp.clip(jnp.round(W / (scale + 1e-08)), -1.0, 1.0) * scale
            return W + jax.lax.stop_gradient(q - W)

        def layernorm(x, gamma, beta):
            mu = jnp.mean(x, axis=-1, keepdims=True)
            var = jnp.var(x, axis=-1, keepdims=True)
            return (x - mu) * jax.lax.rsqrt(var + LN_EPS) * gamma + beta
        B, S, D = x.shape
        N = W_syn.shape[0]
        x_flat = x.reshape(-1, D)
        z = x_flat @ ternary_quant(W_syn).T + b_syn
        k = max(1, int(N * (1.0 - TARGET_SPARSITY)))
        topv, _ = jax.lax.top_k(z, k)
        thresh = topv[:, -1:]
        hidden = jnp.where(z >= thresh, jax.nn.relu(z), 0.0)
        out = hidden @ ternary_quant(W_out).T + b_out
        out = out.reshape(B, S, D)
        return layernorm(x + out, gamma, beta)
    x = L0_attn_x
    xn = _layernorm(x, axis=-1)
    x = x + _L0_attn_ref(xn, L0_attn_Wq, L0_attn_Wk, L0_attn_Wv, L0_attn_Wo, L0_attn_rms_w) + _L0_ffn_ref(xn, L0_ffn_W_syn, L0_ffn_b_syn, L0_ffn_W_out, L0_ffn_b_out, L0_ffn_gamma, L0_ffn_beta)
    return x

_drawn_inputs = setup_inputs


def setup_inputs(seed=0):
    import zlib

    import numpy as np

    out = dict(_drawn_inputs(seed))
    spreads = {'L0_attn_rms_w': (1.0, 0.2),
     'L0_ffn_b_syn': (0.0, 0.1),
     'L0_ffn_b_out': (0.0, 0.1),
     'L0_ffn_gamma': (1.0, 0.2),
     'L0_ffn_beta': (0.0, 0.1)}
    factors = {}
    for name, (base, spread) in spreads.items():
        noise = np.random.default_rng([zlib.crc32(name.encode()), seed]).standard_normal(out[name].shape)
        drawn = base * np.exp(spread * noise) if base else spread * noise
        out[name] = jnp.asarray(drawn.astype(out[name].dtype))
    for name, factor in factors.items():
        out[name] = (out[name] * factor).astype(out[name].dtype)
    return out
```

```python
from contextlib import ExitStack

import concourse.bass as bass
from concourse import mybir

F32 = mybir.dt.float32
F16 = mybir.dt.float16
BF16 = mybir.dt.bfloat16
I32 = mybir.dt.int32
ALU = mybir.AluOpType
ACT = mybir.ActivationFunctionType
AX = mybir.AxisListType
PMAX = bass.bass_isa.ReduceOp.max
PADD = bass.bass_isa.ReduceOp.add

P = 128
E = 512
H, DH = 16, 32
HG = H // 4
N = 2048
KB = E // P
NB = N // P
TOPK = max(1, int(N * (1.0 - 0.9)))
NT = 32
CHUNKS = 8
RING = 5
XS = 256.0
LN_EPS = 1e-5
RANKS = 32
AIM = 19.5
SEGS = 16
SEG = N // SEGS
BIG = 3.0e38
FB = 3 + 2 * (TOPK // 8)
assert TOPK % 8 != 0


def build(nc, x, Wq, Wk, Wv, Wo, rms_w, W_syn, b_syn, W_out, b_out, gamma, beta,
          t_rot, t_dmask, t_qdec, t_kdec, t_rc, t_bd, t_keep, t_ident, t_iota, out):
    ctx = ExitStack()
    with ctx:
        def sb(name, shape, dt):
            return ctx.enter_context(nc.sbuf_tensor(name, shape, dt))[:]

        def pb(name):
            return ctx.enter_context(nc.psum_tensor(name, [P, 512], F32))[:]

        def sem(name):
            return ctx.enter_context(nc.semaphore(name))

        wqkv = sb("wqkv", [P, 2, KB, 3 * E], F16)
        wsynT = sb("wsynT", [P, KB, N], F16)
        woutT = sb("woutT", [P, NB, E], F16)
        wo = sb("wo", [P, KB, E], F32)
        rot = sb("rot", [P, CHUNKS, 3, 8], F32)
        dmask = sb("dmask", [P, H, P], F32)
        qdec = sb("qdec", [P, HG, P], F32)
        kdec = sb("kdec", [P, H], F32)
        rc = sb("rc", [P, E], F32)
        bd = sb("bd", [P, E], F32)
        keep = sb("keep", [P, CHUNKS], F32)
        ident = sb("ident", [P, P], F32)
        iota = sb("iota", [P, RANKS], F32)
        ones = sb("ones", [P, 1], F32)
        gb = sb("gb", [P, N], F32)
        boutx = sb("boutx", [P, E], F32)
        gam = sb("gam", [P, E], F32)
        bet = sb("bet", [P, E], F32)
        area1 = sb("area1", [P, 4 * N], F32)
        z = area1[:, 0:2 * N].rearrange("p (r n) -> p r n", r=2)
        masked = area1[:, 2 * N:3 * N]
        hT = area1[:, 3 * N:4 * N].bitcast(F16).rearrange("p (b t) -> p b t", t=P)
        area2 = sb("area2", [P, 3 * KB * E], F32)
        BQ = area2[:, 0:2048].rearrange("p (g j c) -> p g j c", g=HG, j=4)
        Pr = area2[:, 2048:3072].rearrange("p (r j c) -> p r j c", r=2, j=4)
        qk = area2[:, 3072:5120].rearrange("p (r n) -> p r n", r=2)
        v = area2[:, 5120:6144].rearrange("p (r n) -> p r n", r=2)
        kT = sb("kT", [P, HG, P], F32)
        vd = sb("vd", [P, E], F32)
        rt = sb("rt", [P, 2 * H * 16], F32)
        mask = sb("mask", [P, N], BF16)
        hl = sb("hl", [P, 2, N], F16)
        xr = sb("xr", [P, RING, E], F32)
        xn = sb("xn", [P, RING, E], F32)
        xhl = sb("xhl", [P, 2, E], F16)
        xT = sb("xT", [P, 2, 2 * KB, P], F16)
        aT = sb("aT", [P, HG, P], F32)
        inter_s = sb("inter_s", [P, HG, P], F32)
        sq = sb("sq", [P, HG, P], F32)
        state = sb("state", [P, E], F32)
        y = sb("y", [P, E], F32)
        kvm = y
        kvs = sq.rearrange("p g c -> p (g c)")
        o = sb("o", [P, E], F32)
        cand = sb("cand", [P, 2, SEGS * 8], F32)
        top = sb("top", [P, RANKS], F32)
        sel = sb("sel", [P, RANKS], F32)
        st6 = sb("st6", [P, 2, 6], F32)
        seed6 = sb("seed6", [P, 4, 6], F32)
        c = sb("c", [P, 64], F32)
        names = {}

        def col(name, n=1):
            k = names.setdefault(name, sum(m for m in widths.values()))
            widths.setdefault(name, n)
            return c[:, k:k + n]

        widths = {}
        mv, ve, rstd, r256 = col("mv", 2), col("ve"), col("rstd"), col("r256")
        mvD, veD, rstdD, rD = col("mvD", 2), col("veD"), col("rstdD"), col("rD")
        veR, rstdR = col("veR"), col("rstdR")
        mhalf, half = col("mhalf"), col("half")
        nt0, nt1, pre, t2 = col("nt0"), col("nt1"), col("pre"), col("t2")
        s1, s2, clt, rank, val, m8, fail, thr = (col(k) for k in ("s1", "s2", "clt", "rank", "val", "m8", "fail", "thr"))
        ndh, off, vq = col("ndh"), col("off"), col("vq")
        gs, so, down = col("gs"), col("so"), col("down", 3)
        fb8 = col("fb8", 8)
        failint = sb("failint", [P, 1], I32)
        pc = sb("pc", [P, 64], F32)
        rmsw = sb("rmsw", [P, KB], F32)

        proj = [pb("proj0"), pb("proj1")]
        sring = [pb("sring0"), pb("sring1")]
        p_inter, p_av, p_ffn, p_wo = pb("p_inter"), pb("p_av"), pb("p_ffn"), pb("p_wo")

        S = {k: sem(k) for k in (
            "w_loaded0", "w_loaded1", "w_loaded2", "w_loaded3", "b_loaded", "t_loaded", "wo_loaded",
            "prep_act", "prep_dve", "prep_pool", "tern_done", "ternT0", "ternT1", "w_ready",
            "x_loaded0", "x_loaded1", "ln_stat", "rstd_ready", "r256_ready", "xn_ready", "xh_ready", "xl_ready", "xT_ready",
            "proj_done", "qkv_out", "z_out", "rot_step", "vd_ready", "beta_added", "xnb_ready",
            "qkT_done", "q_blocked", "kT_ready", "scores_done", "P_ready", "inter_done", "av_done",
            "inter_out", "aT_ready", "sq_ready", "kv_done", "ss_done", "veR_ready", "rstdR_ready", "wo_done", "att_added",
            "kvm_ready", "kvs_ready", "state_ready",
            "guess_step", "guess_ready", "sum1", "sum2", "nt_step", "count_done", "w_out", "seg_done", "top_step",
            "fail_ready", "fail_all", "general", "thr_ready", "h_ready", "hi_ready", "lo_ready", "hiT", "loT",
            "ffn_done", "y_ready", "yst", "rstdD_ready", "yg_ready", "out_ready", "out_stored", "seed", "passed")}

        block = ctx.enter_context(nc.Block())

        class Tile:

            def __init__(self, i, k):
                self.n = i * 2 + k
                self.par = k % 2
                self.half = i + k // 2
                self.known = isinstance(i, int)

        def wait(eng, name, tile, per, n):
            value = tile.n * per + n
            if tile.known and value <= 0:
                return
            eng.wait_ge(S[name], value)

        def apart(eng):
            eng.sem_inc(S["passed"], 1)

        def slot(ring, t):
            return ring[:, bass.ds(t.n % RING, 1), :].rearrange("p a n -> p (a n)") if not t.known else ring[:, t.n % RING, :]

        def run_steps(eng, step):
            for s in range(-2, 2):
                step(eng, s // 2, s % 2)
            with eng.Fori(1, NT // 2 - 1) as i:
                step(eng, i, 0)
                step(eng, i, 1)
            for s in range(NT - 2, NT + 2):
                step(eng, s // 2, s % 2)

        def stage(i, p, k):
            t = Tile(i, p + k)
            return t if not t.known or 0 <= t.n < NT else None

        @block.sync
        def _(sp):
            ws = W_syn.rearrange("(b p) d -> p b d", p=P)
            a1 = area1.rearrange("p (b d) -> p b d", d=E)
            a2 = area2.rearrange("p (m b d) -> p m b d", m=3, b=KB)
            for q in range(4):
                sp.dma_start(a1[:, 4 * q:4 * q + 4, :], ws[:, 4 * q:4 * q + 4, :]).then_inc(S[f"w_loaded{q}"], 16)
            for m, W in enumerate((Wq, Wk, Wv)):
                sp.dma_start(a2[:, m], W.rearrange("(b p) n -> p b n", p=P)).then_inc(S["t_loaded"], 16)
            for q in range(4):
                sp.wait_ge(S["tern_done"], q + 1)
                for b in range(4):
                    sp.dma_start_transpose(wsynT[:, :, (4 * q + b) * P:(4 * q + b + 1) * P],
                                           hl[:, q % 2, b * E:(b + 1) * E]).then_inc(S[f"ternT{q % 2}"], 16)
            wt = W_out.rearrange("(b p) n -> p b n", p=P)
            a1o = area1.rearrange("p (b n) -> p b n", n=N)
            for q in range(4):
                sp.dma_start(a1o[:, q, :], wt[:, q, :]).then_inc(S[f"w_loaded{q}"], 16)
            for q in range(4):
                sp.wait_ge(S["tern_done"], 4 + q + 1)
                sp.dma_start_transpose(woutT[:, :, q * P:(q + 1) * P], hl[:, q % 2, :]).then_inc(S[f"ternT{q % 2}"], 16)

            def step(sp, i, p):
                a, u, d = stage(i, p, 2), stage(i, p, -1), stage(i, p, -2)
                if a:
                    wait(sp, "out_ready", a, 1, -RING + 1)
                    apart(sp)
                    sp.dma_start(slot(xr, a), x[bass.ds(a.n * P, P), :] if not a.known else x[a.n * P:(a.n + 1) * P, :]
                                 ).then_inc(S[f"x_loaded{a.par}"], 16)
                if u:
                    wait(sp, "hi_ready", u, 1, 1)
                    apart(sp)
                    wait(sp, "ffn_done", u, 1, 0)
                    apart(sp)
                    sp.dma_start_transpose(hT[:, 0:NB, :], hl[:, 0, :]).then_inc(S["hiT"], 16)
                if a:
                    wait(sp, "xh_ready", a, 1, 1)
                    apart(sp)
                    wait(sp, "xl_ready", a, 1, 1)
                    apart(sp)
                    wait(sp, "proj_done", a, 7, -7)
                    apart(sp)
                    sp.dma_start_transpose(xT[:, a.par], xhl.rearrange("p a n -> p (a n)")).then_inc(S["xT_ready"], 16)
                if u:
                    wait(sp, "lo_ready", u, 1, 1)
                    apart(sp)
                    sp.dma_start_transpose(hT[:, NB:2 * NB, :], hl[:, 1, :]).then_inc(S["loT"], 16)
                if d:
                    wait(sp, "out_ready", d, 1, 1)
                    apart(sp)
                    sp.dma_start(out[bass.ds(d.n * P, P), :] if not d.known else out[d.n * P:(d.n + 1) * P, :], o
                                 ).then_inc(S["out_stored"], 16)

            run_steps(sp, step)
            sp.wait_ge(S["out_stored"], 16 * NT)

        @block.scalar
        def _(act):
            def load(dst, src, name):
                act.dma_start(dst, src).then_inc(S[name], 16)

            load(gb, b_syn.rearrange("(a n) -> a n", a=1).broadcast_to([P, N]), "b_loaded")
            load(boutx, b_out.rearrange("(a n) -> a n", a=1).broadcast_to([P, E]), "b_loaded")
            load(gam, gamma.rearrange("(a n) -> a n", a=1).broadcast_to([P, E]), "b_loaded")
            load(bet, beta.rearrange("(a n) -> a n", a=1).broadcast_to([P, E]), "b_loaded")
            load(wo, Wo.rearrange("(b p) n -> p b n", p=P), "wo_loaded")
            load(rmsw, rms_w, "wo_loaded")
            load(rot, t_rot, "wo_loaded")
            load(dmask, t_dmask, "wo_loaded")
            load(qdec, t_qdec, "wo_loaded")
            load(kdec, t_kdec, "wo_loaded")
            load(rc, t_rc, "wo_loaded")
            load(bd, t_bd, "wo_loaded")
            load(keep, t_keep, "wo_loaded")
            load(ident, t_ident, "wo_loaded")
            load(iota, t_iota, "wo_loaded")

            for w in range(2):
                for q in range(4):
                    act.wait_ge(S[f"w_loaded{q}"], 16 * (w + 1))
                    if w or q:
                        act.wait_ge(S["prep_act"], 4 * w + q)
                    if w and not q:
                        act.wait_ge(S["tern_done"], 4)
                    nc.scalar.activation(mask, area1[:, q * N:(q + 1) * N], ACT.Abs,
                                         accum_out=pc[:, 4 * w + q:4 * w + q + 1]).then_inc(S["prep_act"], 1)
            for m in range(3):
                act.wait_ge(S["prep_dve"], 2 + m)
                nc.scalar.activation(wqkv[:, 0, :, m * E:(m + 1) * E],
                                     area2.rearrange("p (m b d) -> p m b d", m=3, b=KB)[:, m],
                                     ACT.Copy).then_inc(S["prep_act"], 1)

            def step(act, i, p):
                a, b, t, u = stage(i, p, 2), stage(i, p, 1), stage(i, p, 0), stage(i, p, -1)
                if t:
                    wait(act, "guess_ready", t, 1, 1)
                    wait(act, "z_out", t, 4, 4)
                    wait(act, "w_out", t, 1, 0)
                    nc.scalar.activation(mask, z[:, t.par, :], ACT.Sign, bias=nt0, accum_out=s1).then_inc(S["sum1"], 1)
                    wait(act, "nt_step", t, 5, 2)
                    nc.scalar.activation(mask, z[:, t.par, :], ACT.Sign, bias=nt1, accum_out=s2).then_inc(S["sum2"], 1)
                if u:
                    wait(act, "h_ready", u, 1, 1)
                    wait(act, "hiT", u, 16, 0)
                    nc.scalar.activation(hl[:, 0, :], masked, ACT.Copy).then_inc(S["hi_ready"], 1)
                if a:
                    wait(act, "xn_ready", a, 1, 1)
                    wait(act, "xT_ready", a, 16, 0)
                    nc.scalar.activation(xhl[:, 0, :], slot(xn, a), ACT.Copy).then_inc(S["xh_ready"], 1)
                if t:
                    wait(act, "qkT_done", t, 2, 1)
                    wait(act, "scores_done", t, 4, 0)
                    for j in range(4):
                        r = slice(32 * j, 32 * j + 32)
                        nc.scalar.activation(BQ[r, :, j, :], sring[0][r].rearrange("p (g c) -> p g c", g=HG),
                                             ACT.Copy).then_inc(S["q_blocked"], 1)
                    wait(act, "qkT_done", t, 2, 2)
                    nc.scalar.activation(kT.rearrange("p g c -> p (g c)"), sring[1], ACT.Copy).then_inc(S["kT_ready"], 1)
                if b:
                    for m in range(3):
                        wait(act, "proj_done", b, 7, m + 1)
                        if m == 0:
                            wait(act, "kv_done", b, 1, -1)
                            wait(act, "vd_ready", b, 1, -1)
                        dst = qk[:, b.par, m * E:(m + 1) * E] if m < 2 else v[:, b.par, :]
                        nc.scalar.activation(dst, proj[(b.par + m) % 2], ACT.Copy,
                                             scale=down[:, m:m + 1]).then_inc(S["qkv_out"], 1)
                if t:
                    wait(act, "state_ready", t, 1, 0)
                    wait(act, "aT_ready", t, 1, 1)
                    wait(act, "ss_done", t, 1, 0)
                    nc.scalar.activation(sq, aT, ACT.Square).then_inc(S["sq_ready"], 1)

            run_steps(act, step)

        @block.gpsimd
        def _(pool):
            nc.gpsimd.memset(mhalf, -0.5).then_inc(S["prep_pool"], 1)
            nc.gpsimd.memset(half, 0.5).then_inc(S["prep_pool"], 1)
            nc.gpsimd.memset(ones, 1.0).then_inc(S["prep_pool"], 1)
            nc.gpsimd.memset(state, 0.0).then_inc(S["prep_pool"], 1)
            pool.wait_ge(S["prep_dve"], 1)
            nc.gpsimd.partition_all_reduce(pc[:, 17:18], pc[:, 16:17], P, PADD).then_inc(S["prep_pool"], 1)
            pool.wait_ge(S["w_ready"], 1)
            nc.gpsimd.partition_all_reduce(pc[:, 27:30], pc[:, 24:27], P, PMAX).then_inc(S["prep_pool"], 1)
            pool.wait_ge(S["w_ready"], 2)
            nc.gpsimd.partition_all_reduce(pc[:, 19:20], pc[:, 18:19], P, PADD).then_inc(S["prep_pool"], 1)
            pool.wait_ge(S["wo_loaded"], 11 * 16)
            pool.wait_ge(S["prep_dve"], 8)
            nc.gpsimd.memset(BQ, 0.0).then_inc(S["prep_pool"], 1)

            def step(pool, i, p):
                a, b, t, u, d = (stage(i, p, k) for k in (2, 1, 0, -1, -2))
                if t:
                    wait(pool, "qkv_out", t, 3, 3)
                    wait(pool, "kv_done", t, 1, 0)
                    nc.gpsimd.tensor_tensor(vd.rearrange("p (h e) -> p h e", h=H),
                                            v[:, t.par, :].rearrange("p (h e) -> p h e", h=H),
                                            kdec.unsqueeze(2).to_broadcast([P, H, DH]), ALU.mult).then_inc(S["vd_ready"], 1)
                if u:
                    wait(pool, "veR_ready", u, 1, 1)
                    nc.gpsimd.tensor_tensor(rstdR, veR, mhalf, ALU.pow).then_inc(S["rstdR_ready"], 1)
                    wait(pool, "kvs_ready", u, 1, 1)
                    nc.gpsimd.tensor_tensor(state, kvs, kvm, ALU.add).then_inc(S["state_ready"], 1)
                if a:
                    wait(pool, "ln_stat", a, 3, 3)
                    nc.gpsimd.tensor_tensor(rstd, ve, mhalf, ALU.pow).then_inc(S["rstd_ready"], 1)
                if u:
                    wait(pool, "hi_ready", u, 1, 1)
                    wait(pool, "loT", u, 16, 0)
                    nc.gpsimd.tensor_tensor(hl[:, 1, :], masked, hl[:, 0, :], ALU.subtract).then_inc(S["lo_ready"], 1)
                if d:
                    wait(pool, "yst", d, 3, 3)
                    nc.gpsimd.tensor_tensor(rstdD, veD, mhalf, ALU.pow).then_inc(S["rstdD_ready"], 1)
                if t:
                    wait(pool, "count_done", t, 1, 1)
                    if u:
                        wait(pool, "lo_ready", u, 1, 1)
                    nc.gpsimd.tensor_tensor(masked, z[:, t.par, :], mask, ALU.mult).then_inc(S["w_out"], 1)
                if a:
                    wait(pool, "xh_ready", a, 1, 1)
                    apart(pool)
                    nc.gpsimd.tensor_tensor(xhl[:, 1, :], slot(xn, a), xhl[:, 0, :], ALU.subtract).then_inc(S["xl_ready"], 1)
                    wait(pool, "xl_ready", a, 1, 1)
                    apart(pool)
                    nc.gpsimd.tensor_tensor(slot(xn, a), slot(xn, a), boutx, ALU.add).then_inc(S["xnb_ready"], 1)
                    apart(pool)
                    nc.gpsimd.tensor_tensor(slot(xr, a), slot(xr, a), bet, ALU.add).then_inc(S["beta_added"], 1)
                if b:
                    wait(pool, "qkv_out", b, 3, 2)
                    ch = b.n % CHUNKS
                    trig = (rot[:, bass.ds(ch, 1)].rearrange("p a f e -> p (a f) e") if not b.known else rot[:, ch])
                    q4 = qk[:, b.par, :].rearrange("p (h a e) -> p h a e", a=2, e=16)
                    r4 = rt.rearrange("p (h a e) -> p h a e", a=2, e=8)
                    cos = trig[:, 0, :].unsqueeze(1).unsqueeze(1).to_broadcast([P, 2 * H, 2, 8])
                    for a_ in range(2):
                        sn = trig[:, 1 + a_, :].unsqueeze(1).to_broadcast([P, 2 * H, 8])
                        apart(pool)
                        nc.gpsimd.tensor_tensor(r4[:, :, a_], q4[:, :, 1 - a_, 0:8], sn,
                                                ALU.mult).then_inc(S["rot_step"], 1)
                    wait(pool, "rot_step", b, 4, 2)
                    apart(pool)
                    nc.gpsimd.tensor_tensor(q4[:, :, :, 0:8], q4[:, :, :, 0:8], cos, ALU.mult).then_inc(S["rot_step"], 1)
                    wait(pool, "rot_step", b, 4, 3)
                    nc.gpsimd.tensor_tensor(q4[:, :, :, 0:8], q4[:, :, :, 0:8], r4, ALU.add).then_inc(S["rot_step"], 1)
                if t:
                    wait(pool, "fail_ready", t, 1, 1)
                    apart(pool)
                    nc.gpsimd.partition_all_reduce(failint, fail, P, PMAX).then_inc(S["fail_all"], 1)

            run_steps(pool, step)

        @block.tensor
        def _(pe):
            pe.wait_ge(S["prep_dve"], 8)
            pe.wait_ge(S["prep_pool"], 8)
            for q in range(2):
                pe.wait_ge(S[f"ternT{q}"], 160)

            def step(pe, i, p):
                b, t, u, d = (stage(i, p, k) for k in (1, 0, -1, -2))

                def projection(n):
                    wait(pe, "xT_ready", b, 16, 16)
                    if n < 2:
                        wait(pe, "z_out", b, 4, n - 1)
                    elif n < 5:
                        wait(pe, "qkv_out", b, 3, n - 1)
                    else:
                        wait(pe, "z_out", b, 4, n - 4)
                    if n < 3:
                        pairs = [(k + KB * l, wqkv[:, w, k, n * E:(n + 1) * E]) for k in range(KB)
                                 for l, w in ((0, 0), (0, 1), (1, 0))]
                    else:
                        pairs = [(k, wsynT[:, k % KB, (n - 3) * 512:(n - 2) * 512]) for k in range(2 * KB)]
                    bank = proj[(b.par + n) % 2]
                    for m, (k, w) in enumerate(pairs):
                        last = nc.tensor.matmul(bank, xT[:, b.par, k, :], w, start=m == 0, stop=m == len(pairs) - 1)
                    last.then_inc(S["proj_done"], 1)

                def scores(g):
                    wait(pe, "q_blocked", t, 4, 4)
                    wait(pe, "kT_ready", t, 1, 1)
                    if g >= 2:
                        wait(pe, "P_ready", t, 4, g - 1)
                    nc.tensor.matmul(sring[g % 2], kT[:, g, :], BQ[:, g].rearrange("p j c -> p (j c)"),
                                     start=True, stop=True).then_inc(S["scores_done"], 1)

                def values(g):
                    wait(pe, "P_ready", t, 4, g + 1)
                    if g == 0:
                        wait(pe, "aT_ready", t, 1, 0)
                    for j in range(4):
                        h = 4 * g + j
                        last = nc.tensor.matmul(p_av[32 * j:32 * j + 32, g * P:(g + 1) * P],
                                                v[:, t.par, h * DH:(h + 1) * DH], Pr[:, g % 2, j, :],
                                                start=True, stop=True)
                    last.then_inc(S["av_done"], 1)

                if d:
                    wait(pe, "hiT", d, 16, 16)
                    wait(pe, "y_ready", d, 1, 0)
                    for k in range(2 * NB):
                        if k == NB:
                            wait(pe, "loT", d, 16, 16)
                        last = nc.tensor.matmul(p_ffn, hT[:, k, :], woutT[:, k % NB, :], start=k == 0,
                                                stop=k == 2 * NB - 1)
                    last.then_inc(S["ffn_done"], 1)
                if t:
                    wait(pe, "rot_step", t, 4, 4)
                    if t.known:
                        pe.wait_ge(S["wo_loaded"], 11 * 16)
                    for m in range(2):
                        if m == 0:
                            wait(pe, "kvm_ready", t, 1, 0)
                        else:
                            wait(pe, "veR_ready", t, 1, 0)
                        for g in range(HG):
                            last = nc.tensor.transpose(sring[m][:, g * P:(g + 1) * P],
                                                       qk[:, t.par, m * E + g * P:m * E + (g + 1) * P], ident)
                        last.then_inc(S["qkT_done"], 1)
                if b:
                    for n in range(3):
                        projection(n)
                if t:
                    wait(pe, "q_blocked", t, 4, 4)
                    wait(pe, "state_ready", t, 1, 0)
                    wait(pe, "inter_out", t, 1, 0)
                    for g in range(HG):
                        for j in range(4):
                            last = nc.tensor.matmul(p_inter[32 * j:32 * j + 32, g * P:(g + 1) * P],
                                                    state[:, g * P + 32 * j:g * P + 32 * j + 32],
                                                    BQ[:, g, j, :], start=True, stop=True)
                    last.then_inc(S["inter_done"], 1)
                    scores(0)
                    scores(1)
                if b:
                    projection(3)
                if t:
                    values(0)
                    scores(2)
                    values(1)
                    scores(3)
                if b:
                    projection(4)
                if t:
                    values(2)
                    values(3)
                if b:
                    projection(5)
                if t:
                    wait(pe, "vd_ready", t, 1, 1)
                    wait(pe, "P_ready", t, 4, 3)
                    for g in range(HG):
                        last = nc.tensor.matmul(sring[0][:, g * P:(g + 1) * P],
                                                qk[:, t.par, E + g * P:E + (g + 1) * P],
                                                vd[:, g * P:(g + 1) * P], start=True, stop=True)
                    last.then_inc(S["kv_done"], 1)
                if b:
                    projection(6)
                if t:
                    wait(pe, "sq_ready", t, 1, 1)
                    wait(pe, "P_ready", t, 4, 4)
                    for g in range(HG):
                        last = nc.tensor.matmul(sring[1][:, 0:1], sq[:, g, :], ones, start=g == 0, stop=g == HG - 1)
                    last.then_inc(S["ss_done"], 1)
                    wait(pe, "att_added", t, 1, 0)
                    for g in range(HG):
                        last = nc.tensor.matmul(p_wo, aT[:, g, :], wo[:, g, :], start=g == 0, stop=g == HG - 1)
                    last.then_inc(S["wo_done"], 1)

            run_steps(pe, step)

        @block.vector
        def _(dve):
            done = [0]

            def then(ins):
                done[0] += 1
                ins.then_inc(S["seed"], 1)
                dve.wait_ge(S["seed"], done[0])

            def pow2(dst, src):
                then(nc.vector.tensor_scalar(dst.bitcast(I32), src.bitcast(I32), 0x7F800000, None, ALU.bitwise_and))

            def ternary(w, q, lo, hi):
                src = area1[:, q * N:(q + 1) * N]
                n = 4 * w + q
                if n >= 2:
                    dve.wait_ge(S[f"ternT{q % 2}"], 64 * (n // 2) if n < 6 else 144)
                then(nc.vector.tensor_scalar(mask, src, lo, None, ALU.is_lt))
                nc.vector.scalar_tensor_tensor(hl[:, q % 2, :], src, hi, mask, ALU.is_gt,
                                               ALU.subtract).then_inc(S["tern_done"], 1)
                dve.wait_ge(S["tern_done"], n + 1)

            dve.wait_ge(S["prep_act"], 4)
            nc.vector.reduce_sum(pc[:, 16:17], pc[:, 0:4], AX.X).then_inc(S["prep_dve"], 1)
            dve.wait_ge(S["prep_pool"], 5)
            scale_syn = pc[:, 20:21]
            then(nc.vector.tensor_scalar(scale_syn, pc[:, 17:18], 1.0 / (N * E), None, ALU.mult))
            then(nc.vector.tensor_scalar(pc[:, 21:22], scale_syn, 1e-8, 0.5, ALU.add, ALU.mult))
            then(nc.vector.tensor_scalar(pc[:, 22:23], pc[:, 21:22], -1.0, None, ALU.mult))
            for q in range(4):
                ternary(0, q, pc[:, 22:23], pc[:, 21:22])
            a2 = area2.rearrange("p (m n) -> p m n", m=3)
            dve.wait_ge(S["t_loaded"], 48)
            then(nc.vector.tensor_reduce(pc[:, 24:27], a2, AX.X, ALU.max))
            then(nc.vector.tensor_reduce(pc[:, 30:33], a2, AX.X, ALU.min))
            then(nc.vector.tensor_scalar(pc[:, 30:33], pc[:, 30:33], -1.0, None, ALU.mult))
            nc.vector.tensor_tensor(pc[:, 24:27], pc[:, 24:27], pc[:, 30:33], ALU.max).then_inc(S["w_ready"], 1)
            dve.wait_ge(S["prep_pool"], 6)
            then(nc.vector.tensor_scalar(pc[:, 27:30], pc[:, 27:30], 1e-30, None, ALU.max))
            pow2(pc[:, 33:36], pc[:, 27:30])
            then(nc.vector.reciprocal(pc[:, 36:39], pc[:, 33:36]))
            then(nc.vector.tensor_scalar(pc[:, 36:39], pc[:, 36:39], 256.0, None, ALU.mult))
            then(nc.vector.tensor_scalar(down, pc[:, 33:36], 1.0 / (256.0 * XS), None, ALU.mult))
            for m in range(3):
                nc.vector.tensor_scalar(a2[:, m], a2[:, m], pc[:, 36 + m:37 + m], None, ALU.mult).then_inc(S["prep_dve"], 1)
            for m in range(3):
                dve.wait_ge(S["prep_act"], 8 + m + 1)
                dve.wait_ge(S["prep_dve"], 2 + m)
                w4 = area2.rearrange("p (m b d) -> p m b d", m=3, b=KB)[:, m]
                nc.vector.tensor_tensor(wqkv[:, 1, :, m * E:(m + 1) * E], w4, wqkv[:, 0, :, m * E:(m + 1) * E],
                                        ALU.subtract).then_inc(S["prep_dve"], 1)
            dve.wait_ge(S["b_loaded"], 64)
            then(nc.vector.tensor_reduce(pc[:, 40:41], gb, AX.X, ALU.max))
            then(nc.vector.tensor_reduce(pc[:, 41:42], gb, AX.X, ALU.min))
            then(nc.vector.tensor_scalar(pc[:, 41:42], pc[:, 41:42], -1.0, None, ALU.mult))
            then(nc.vector.tensor_tensor(pc[:, 40:41], pc[:, 40:41], pc[:, 41:42], ALU.max))
            then(nc.vector.scalar_tensor_tensor(pc[:, 42:43], scale_syn, float(E), pc[:, 40:41], ALU.mult, ALU.add))
            then(nc.vector.tensor_scalar(pc[:, 42:43], pc[:, 42:43], 1e-30, None, ALU.max))
            pow2(pc[:, 43:44], pc[:, 42:43])
            then(nc.vector.reciprocal(pc[:, 44:45], pc[:, 43:44]))
            then(nc.vector.tensor_scalar(pc[:, 44:45], pc[:, 44:45], 16384.0, None, ALU.mult))
            then(nc.vector.scalar_tensor_tensor(gs, scale_syn, 1.0 / XS, pc[:, 44:45], ALU.mult, ALU.mult))
            then(nc.vector.tensor_scalar(gb, gb, pc[:, 44:45], None, ALU.mult))
            then(nc.vector.tensor_scalar(boutx, boutx, XS, None, ALU.mult))
            dve.wait_ge(S["wo_loaded"], 11 * 16)
            for k in range(KB):
                then(nc.vector.tensor_scalar(wo[:, k, :], wo[:, k, :], rmsw[:, k:k + 1], None, ALU.mult))
            dve.wait_ge(S["prep_act"], 8)
            nc.vector.reduce_sum(pc[:, 18:19], pc[:, 4:8], AX.X).then_inc(S["w_ready"], 1)
            dve.wait_ge(S["prep_pool"], 7)
            then(nc.vector.tensor_scalar(pc[:, 45:46], pc[:, 19:20], 1.0 / (N * E), None, ALU.mult))
            then(nc.vector.tensor_scalar(pc[:, 46:47], pc[:, 45:46], 1e-8, 0.5, ALU.add, ALU.mult))
            then(nc.vector.tensor_scalar(pc[:, 47:48], pc[:, 46:47], -1.0, None, ALU.mult))
            then(nc.vector.scalar_tensor_tensor(so, pc[:, 45:46], XS / 16384.0, pc[:, 43:44], ALU.mult, ALU.mult))
            for q in range(4):
                ternary(1, q, pc[:, 47:48], pc[:, 46:47])
            nc.vector.tensor_scalar(pc[:, 48:49], pc[:, 47:48], 0.0, None, ALU.mult).then_inc(S["prep_dve"], 1)

            def step(dve, i, p):
                a, b, t, u, d = (stage(i, p, k) for k in (2, 1, 0, -1, -2))

                def probs(g):
                    wait(dve, "scores_done", t, 4, g + 1)
                    wait(dve, "av_done", t, 4, g - 1)
                    nc.vector.tensor_tensor(Pr[:, g % 2], sring[g % 2].rearrange("p (j c) -> p j c", j=4),
                                            dmask[:, 4 * g:4 * g + 4, :], ALU.mult).then_inc(S["P_ready"], 1)

                def z_chunk(n):
                    wait(dve, "proj_done", b, 7, 4 + n)
                    if n == 0:
                        wait(dve, "h_ready", b, 1, -1)
                    nc.vector.scalar_tensor_tensor(z[:, b.par, n * 512:(n + 1) * 512], proj[(b.par + 3 + n) % 2], gs,
                                                   gb[:, n * 512:(n + 1) * 512], ALU.mult, ALU.add).then_inc(S["z_out"], 1)

                def segments(k):
                    wait(dve, "w_out", t, 1, 1)
                    wait(dve, "top_step", t, 12, 0)
                    for n in range(4 * k, 4 * k + 4):
                        apart(dve)
                        nc.vector.max(cand[:, 0, 8 * n:8 * n + 8], masked[:, n * SEG:(n + 1) * SEG]).then_inc(S["seg_done"], 1)

                if u:
                    wait(dve, "kv_done", u, 1, 1)
                    wait(dve, "state_ready", u, 1, 0)
                    wait(dve, "out_ready", u, 1, -1)
                    ch = u.n % CHUNKS
                    kp = keep[:, bass.ds(ch, 1)] if not u.known else keep[:, ch:ch + 1]
                    nc.vector.scalar_tensor_tensor(kvm, sring[0], kp, bd, ALU.mult, ALU.mult).then_inc(S["kvm_ready"], 1)
                    wait(dve, "ss_done", u, 1, 1)
                    nc.vector.scalar_tensor_tensor(kvs, state, kp, rc, ALU.mult, ALU.mult).then_inc(S["kvs_ready"], 1)
                    nc.vector.tensor_scalar(veR, sring[1][:, 0:1], 1.0 / E, LN_EPS, ALU.mult, ALU.add).then_inc(S["veR_ready"], 1)
                    wait(dve, "fail_all", u, 1, 1)
                    apart(dve)
                    missed = dve.value_load(failint[0:1, 0:1])
                    with dve.If(missed > 0):
                        wait(dve, "seg_done", u, 16, 16)
                        nc.vector.tensor_copy(masked, z[:, u.par, :]).then_inc(S["general"], 1)
                        with dve.Fori(0, TOPK // 8) as r:
                            dve.wait_ge(S["general"], u.n * FB + r * 2 + 1)
                            apart(dve)
                            nc.vector.max(fb8, masked).then_inc(S["general"], 1)
                            dve.wait_ge(S["general"], u.n * FB + r * 2 + 2)
                            apart(dve)
                            nc.vector.match_replace(masked, fb8, masked, -BIG).then_inc(S["general"], 1)
                        dve.wait_ge(S["general"], u.n * FB + FB - 2)
                        apart(dve)
                        nc.vector.max(fb8, masked).then_inc(S["general"], 1)
                        dve.wait_ge(S["general"], u.n * FB + FB - 1)
                        nc.vector.tensor_copy(val, fb8[:, TOPK % 8 - 1:TOPK % 8]).then_inc(S["general"], 1)
                    with dve.Else():
                        dve.sem_inc(S["general"], FB)
                    dve.wait_ge(S["general"], u.n * FB + FB)
                    nc.vector.tensor_scalar(thr, val, 0.0, None, ALU.max).then_inc(S["thr_ready"], 1)
                    nc.vector.tensor_scalar(vq, val, -0.25, None, ALU.mult).then_inc(S["guess_step"], 1)
                    wait(dve, "guess_step", u, 1, 1)
                    nc.vector.scalar_tensor_tensor(nt0, nt0, 0.75, vq, ALU.mult, ALU.add).then_inc(S["guess_ready"], 1)
                    wait(dve, "thr_ready", u, 1, 1)
                    nc.vector.scalar_tensor_tensor(masked, z[:, u.par, :], thr, z[:, u.par, :], ALU.is_ge,
                                                   ALU.mult).then_inc(S["h_ready"], 1)
                if a:
                    dve.wait_ge(S[f"x_loaded{a.par}"], a.half * 16 + 16)
                    nc.vector.bn_stats(st6[:, 0, :], slot(xr, a)).then_inc(S["ln_stat"], 1)
                    wait(dve, "ln_stat", a, 3, 1)
                    apart(dve)
                    nc.vector.bn_aggr(mv, st6[:, 0:1, :]).then_inc(S["ln_stat"], 1)
                    wait(dve, "ln_stat", a, 3, 2)
                    nc.vector.tensor_scalar(ve, mv[:, 1:2], LN_EPS, None, ALU.add).then_inc(S["ln_stat"], 1)
                if t and t.known and t.n == 0:
                    wait(dve, "z_out", t, 4, 4)
                    for n in range(4):
                        then(nc.vector.bn_stats(seed6[:, n, :], z[:, 0, n * 512:(n + 1) * 512]))
                    then(nc.vector.bn_aggr(pc[:, 50:52], seed6))
                    then(nc.vector.tensor_scalar(pc[:, 52:53], pc[:, 51:52], 1e-30, None, ALU.max))
                    then(nc.vector.reciprocal(pc[:, 53:54], pc[:, 52:53]))
                    then(nc.vector.tensor_copy(pc[:, 54:55], pc[:, 53:54]))
                    then(nc.vector.tensor_scalar(pc[:, 55:56], pc[:, 52:53], 1.0, 0.5, ALU.add, ALU.mult))
                    for _ in range(12):
                        then(nc.vector.reciprocal(pc[:, 54:55], pc[:, 55:56]))
                        then(nc.vector.tensor_tensor(pc[:, 54:55], pc[:, 54:55], pc[:, 52:53], ALU.mult))
                        then(nc.vector.tensor_tensor(pc[:, 55:56], pc[:, 55:56], pc[:, 54:55], ALU.add))
                        then(nc.vector.tensor_scalar(pc[:, 55:56], pc[:, 55:56], 0.5, None, ALU.mult))
                    then(nc.vector.tensor_scalar(ndh, pc[:, 55:56], -0.5 / 359.4, None, ALU.mult))
                    then(nc.vector.tensor_scalar(off, pc[:, 55:56], 0.5 / 359.4 * (N - 2 * (TOPK - AIM)), None, ALU.mult))
                    then(nc.vector.tensor_scalar(pc[:, 56:57], pc[:, 50:51], -1.0, None, ALU.mult))
                    nc.vector.scalar_tensor_tensor(nt0, pc[:, 55:56], -1.2816, pc[:, 56:57], ALU.mult,
                                                   ALU.add).then_inc(S["guess_ready"], 1)
                if u:
                    wait(dve, "wo_done", u, 1, 1)
                    wait(dve, "rstdR_ready", u, 1, 1)
                    wait(dve, "beta_added", u, 1, 1)
                    nc.vector.scalar_tensor_tensor(slot(xr, u), p_wo, rstdR, slot(xr, u), ALU.mult,
                                                   ALU.add).then_inc(S["att_added"], 1)
                if t:
                    wait(dve, "guess_ready", t, 1, 1)
                    nc.vector.tensor_scalar(pre, nt0, off, None, ALU.subtract).then_inc(S["nt_step"], 1)
                    wait(dve, "sum1", t, 1, 1)
                    wait(dve, "nt_step", t, 5, 1)
                    nc.vector.tensor_scalar(nt1, s1, ndh, pre, ALU.mult, ALU.add).then_inc(S["nt_step"], 1)
                if a:
                    wait(dve, "rstd_ready", a, 1, 1)
                    nc.vector.tensor_scalar(r256, rstd, XS, None, ALU.mult).then_inc(S["r256_ready"], 1)
                    wait(dve, "r256_ready", a, 1, 1)
                    nc.vector.tensor_scalar(slot(xn, a), slot(xr, a), mv[:, 0:1], r256, ALU.subtract,
                                            ALU.mult).then_inc(S["xn_ready"], 1)
                if t:
                    wait(dve, "nt_step", t, 5, 2)
                    nc.vector.tensor_scalar(pre, nt1, off, None, ALU.subtract).then_inc(S["nt_step"], 1)
                    wait(dve, "sum2", t, 1, 1)
                    wait(dve, "nt_step", t, 5, 3)
                    nc.vector.tensor_scalar(pre, s2, ndh, pre, ALU.mult, ALU.add).then_inc(S["nt_step"], 1)
                    wait(dve, "nt_step", t, 5, 4)
                    nc.vector.tensor_scalar(t2, pre, -1.0, None, ALU.mult).then_inc(S["nt_step"], 1)
                    wait(dve, "nt_step", t, 5, 5)
                    nc.vector.tensor_scalar(mask, z[:, t.par, :], t2, 0.0, ALU.is_lt, ALU.add,
                                            accum_out=clt).then_inc(S["count_done"], 1)
                if d:
                    wait(dve, "ffn_done", d, 1, 1)
                    wait(dve, "xnb_ready", d, 1, 1)
                    wait(dve, "out_ready", d, 1, 0)
                    wait(dve, "state_ready", d, 1, 2 if u else 1)
                    nc.vector.scalar_tensor_tensor(y, p_ffn, so, slot(xn, d), ALU.mult, ALU.add).then_inc(S["y_ready"], 1)
                    wait(dve, "y_ready", d, 1, 1)
                    nc.vector.bn_stats(st6[:, 1, :], y).then_inc(S["yst"], 1)
                    wait(dve, "yst", d, 3, 1)
                    apart(dve)
                    nc.vector.bn_aggr(mvD, st6[:, 1:2, :]).then_inc(S["yst"], 1)
                    wait(dve, "yst", d, 3, 2)
                    nc.vector.tensor_scalar(veD, mvD[:, 1:2], 1.0 / (XS * XS), LN_EPS, ALU.mult, ALU.add).then_inc(S["yst"], 1)
                    nc.vector.scalar_tensor_tensor(y, y, mvD[:, 0:1], gam, ALU.subtract, ALU.mult).then_inc(S["yg_ready"], 1)
                    wait(dve, "rstdD_ready", d, 1, 1)
                    nc.vector.tensor_scalar(rD, rstdD, 1.0 / XS, None, ALU.mult).then_inc(S["yg_ready"], 1)
                    wait(dve, "yg_ready", d, 2, 2)
                    wait(dve, "out_stored", d, 16, 0)
                    wait(dve, "att_added", d, 1, 1)
                    nc.vector.scalar_tensor_tensor(o, y, rD, slot(xr, d), ALU.mult, ALU.add).then_inc(S["out_ready"], 1)
                if t:
                    probs(0)
                    segments(0)
                    probs(1)
                if b:
                    z_chunk(0)
                if t:
                    segments(1)
                    probs(2)
                    segments(2)
                    probs(3)
                if b:
                    z_chunk(1)
                if t:
                    wait(dve, "inter_done", t, 1, 1)
                    nc.vector.tensor_tensor(inter_s, p_inter.rearrange("p (g c) -> p g c", g=HG), qdec,
                                            ALU.mult).then_inc(S["inter_out"], 1)
                    wait(dve, "inter_out", t, 1, 1)
                    wait(dve, "av_done", t, 4, 4)
                    wait(dve, "wo_done", t, 1, 0)
                    nc.vector.tensor_tensor(aT, p_av.rearrange("p (g c) -> p g c", g=HG), inter_s,
                                            ALU.add).then_inc(S["aT_ready"], 1)
                if b:
                    z_chunk(2)
                if t:
                    segments(3)
                if b:
                    z_chunk(3)
                if t:
                    wait(dve, "count_done", t, 1, 1)
                    nc.vector.tensor_scalar(rank, clt, float(TOPK - N), None, ALU.add).then_inc(S["top_step"], 1)
                    wait(dve, "seg_done", t, 16, 16)
                    nc.vector.tensor_reduce(m8, cand[:, 0, :].rearrange("p (s k) -> p s k", k=8)[:, :, 7], AX.X,
                                            ALU.max).then_inc(S["top_step"], 1)
                    for r in range(RANKS // 8):
                        apart(dve)
                        nc.vector.max(top[:, 8 * r:8 * r + 8], cand[:, r % 2, :]).then_inc(S["top_step"], 1)
                        if r < RANKS // 8 - 1:
                            wait(dve, "top_step", t, 12, 3 + 2 * r)
                            apart(dve)
                            nc.vector.match_replace(cand[:, (r + 1) % 2, :], top[:, 8 * r:8 * r + 8], cand[:, r % 2, :],
                                                    -BIG).then_inc(S["top_step"], 1)
                            wait(dve, "top_step", t, 12, 4 + 2 * r)
                    wait(dve, "top_step", t, 12, 9)
                    nc.vector.scalar_tensor_tensor(sel, iota, rank, top, ALU.is_equal, ALU.mult,
                                                   accum_out=val).then_inc(S["top_step"], 1)
                    wait(dve, "top_step", t, 12, 10)
                    nc.vector.tensor_scalar(pre, val, 0.0, None, ALU.is_le).then_inc(S["top_step"], 1)
                    nc.vector.tensor_tensor(s1, m8, val, ALU.is_gt).then_inc(S["top_step"], 1)
                    wait(dve, "top_step", t, 12, 12)
                    nc.vector.tensor_tensor(fail, pre, s1, ALU.max).then_inc(S["fail_ready"], 1)

            run_steps(dve, step)


_INS = ["L0_attn_x", "L0_attn_Wq", "L0_attn_Wk", "L0_attn_Wv", "L0_attn_Wo", "L0_attn_rms_w", "L0_ffn_W_syn",
        "L0_ffn_b_syn", "L0_ffn_W_out", "L0_ffn_b_out", "L0_ffn_gamma", "L0_ffn_beta"]


def tables():
    import numpy as np

    f = np.float32
    freq = (f(1.0 / 1024.0) ** np.linspace(0.0, 1.0, DH // 4, dtype=f)).astype(f)
    theta = (np.arange(CHUNKS * P, dtype=f)[:, None] * freq[None, :]).astype(f).astype(np.float64)
    cos, sin = np.cos(theta), np.sin(theta)
    rot = np.stack([cos, sin, -sin], 1).reshape(CHUNKS, P, 3, 8).transpose(1, 0, 2, 3)
    start = 2.0 ** (-2.0 ** (-(np.log2(H) - 3)))
    slopes = np.array([start * start ** i for i in range(H)]).astype(f)
    r = np.exp(-slopes.astype(np.float64)).astype(f).astype(np.float64)
    i = np.arange(P)
    diff = i[None, :] - i[:, None]
    dmask = np.where(diff[:, None, :] >= 0, r[None, :, None] ** np.maximum(diff, 0)[:, None, :], 0.0)
    rg = r.reshape(HG, 4)
    qdec = np.repeat(rg.T, DH, axis=0)[:, :, None] ** (i[None, None, :] + 1.0)
    kdec = r[None, :] ** (127.0 - i[:, None])
    blocks = np.kron(np.eye(4), np.ones((DH, DH)))
    bd = np.tile(blocks, (1, HG))
    rc = np.concatenate([blocks * np.repeat(rg[g] ** 128.0, DH)[:, None] for g in range(HG)], 1)
    keep = np.tile((np.arange(CHUNKS) < CHUNKS - 1).astype(f), (P, 1))
    iota = np.tile(np.arange(1, RANKS + 1, dtype=f), (P, 1))
    return {k: np.ascontiguousarray(a, dtype=f) for k, a in dict(
        t_rot=rot, t_dmask=dmask, t_qdec=qdec, t_kdec=kdec, t_rc=rc, t_bd=bd, t_keep=keep, t_ident=np.eye(P),
        t_iota=iota).items()}


def kernel(**inputs):
    import numpy as _np
    import concourse.bacc as _bacc
    from concourse import mybir as _mybir
    from concourse.bass_utils import run_bass_kernel_spmd as _run

    nc = _bacc.Bacc("TRN2", target_bir_lowering=False, num_devices=1)
    arrays, args = {}, []
    for name in _INS:
        a = _np.ascontiguousarray(inputs[name])
        if name == "L0_attn_x":
            a = a.reshape(NT * P, E)
        if name == "L0_attn_rms_w":
            a = _np.ascontiguousarray(a.reshape(KB, P).T)
        arrays[f"in_{name}_dram"] = a
        args.append(nc.dram_tensor(f"in_{name}_dram", a.shape, _mybir.dt.from_np(a.dtype), kind="ExternalInput").ap())
    for name, a in tables().items():
        arrays[f"{name}_dram"] = a
        args.append(nc.dram_tensor(f"{name}_dram", a.shape, _mybir.dt.from_np(a.dtype), kind="ExternalInput").ap())
    args.append(nc.dram_tensor("out_0_dram", (NT * P, E), F32, kind="ExternalOutput").ap())
    build(nc, *args)
    r = _run(nc, [arrays], core_ids=[0])
    return r.results[0]["out_0_dram"].reshape(4, NT * P // 4, E)
```

```python
from contextlib import ExitStack

import concourse.bass as bass
from concourse import mybir

F32 = mybir.dt.float32
F16 = mybir.dt.float16
BF16 = mybir.dt.bfloat16
I32 = mybir.dt.int32
ALU = mybir.AluOpType
ACT = mybir.ActivationFunctionType
AX = mybir.AxisListType
PMAX = bass.bass_isa.ReduceOp.max
PADD = bass.bass_isa.ReduceOp.add

P = 128
E = 512
H, DH = 16, 32
HG = H // 4
N = 2048
KB = E // P
NB = N // P
TOPK = max(1, int(N * (1.0 - 0.9)))
NT = 32
CHUNKS = 8
RING = 5
XS = 256.0
WS = 2.0 ** 14
QS = 32.0
LN_EPS = 1e-5
RANKS = 32
AIM = 19.5
SEGS = 16
SEG = N // SEGS
BIG = 3.0e38
BELOW = 1.0 - 2.0 ** -24
FB = 3 + 2 * (TOPK // 8)
assert TOPK % 8 != 0


def build(nc, x, Wq, Wk, Wv, Wo, rms_w, W_syn, b_syn, W_out, b_out, gamma, beta,
          t_rot, t_dmask, t_qdec, t_kdec, t_rc, t_keep, t_ident, t_iota, out):
    ctx = ExitStack()
    with ctx:
        def sb(name, shape, dt):
            return ctx.enter_context(nc.sbuf_tensor(name, shape, dt))[:]

        def pb(name):
            return ctx.enter_context(nc.psum_tensor(name, [P, 512], F32))[:]

        def sem(name):
            return ctx.enter_context(nc.semaphore(name))

        wqkv = sb("wqkv", [P, 2, KB, 3 * E], F16)
        wsynT = sb("wsynT", [P, NB, KB, P], F16)
        woutT = sb("woutT", [P, NB, E], F16)
        wo = sb("wo", [P, KB, E], F32)
        rot = sb("rot", [P, CHUNKS, 3, 8], F32)
        dmask = sb("dmask", [P, H, P], F32)
        qdec = sb("qdec", [P, HG, P], F32)
        kdec = sb("kdec", [P, H], F32)
        rc = sb("rc", [P, CHUNKS, HG], F32)
        keep = sb("keep", [P, CHUNKS], F32)
        ident = sb("ident", [P, P], F32)
        iota = sb("iota", [P, RANKS], F32)
        ones = sb("ones", [P, 1], F32)
        gb = sb("gb", [P, N], F32)
        boutx = sb("boutx", [P, E], F32)
        gam = sb("gam", [P, E], F32)
        bet = sb("bet", [P, E], F32)
        area1 = sb("area1", [P, 4 * N], F32)
        z = area1[:, 0:2 * N].rearrange("p (r n) -> p r n", r=2)
        masked = area1[:, 2 * N:3 * N]
        hT = area1[:, 3 * N:4 * N].bitcast(F16).rearrange("p (b t) -> p b t", t=P)
        area2 = sb("area2", [P, 3 * KB * E], F32)
        qks = area2[:, 2048:4096].bitcast(F16).rearrange("p (m h a d) -> p m h a d", m=2, h=H, a=4)
        qkst = area2[:, 4096:6144].bitcast(F16).rearrange("p (m h c) -> p m h c", m=2, h=H)
        qk = area2[:, 0:2048].rearrange("p (r n) -> p r n", r=2)
        v = sb("v", [P, 2, E], F32)
        Pr = sb("Pr", [P, 2, 4, P], F32)
        unused = Pr.rearrange("p r j c -> p (r j c)").bitcast(F16)
        pair_c = sb("pair_c", [P, 2 * E], F32)
        qTd = pair_c[:, 0:E].rearrange("p (g c) -> p g c", g=HG)
        vd = pair_c[:, E:2 * E]
        rt = sb("rt", [P, 2 * H * 16], F32)
        hl = sb("hl", [P, 2, N], F16)
        xr = sb("xr", [P, RING, E], F32)
        xn = sb("xn", [P, RING, E], F32)
        xhl = sb("xhl", [P, 2, E], F16)
        xT = sb("xT", [P, 2, 2 * KB, P], F16)
        pair_a = sb("pair_a", [P, 2 * E], F32)
        aT = pair_a[:, 0:E].rearrange("p (g c) -> p g c", g=HG)
        sq = pair_a[:, E:2 * E].rearrange("p (g c) -> p g c", g=HG)
        state = sb("state", [P, P], F32)
        stateD = sb("stateD", [P, HG, P], F32)
        kvs = sb("kvs", [P, P], F32)
        pair_b = sb("pair_b", [P, 2 * E], F32)
        y, o = pair_b[:, 0:E], pair_b[:, E:2 * E]
        cand = sb("cand", [P, 2, SEGS * 8], F32)
        top = sb("top", [P, RANKS], F32)
        sel = sb("sel", [P, RANKS], F32)
        st6 = sb("st6", [P, 2, 6], F32)
        seed6 = sb("seed6", [P, 4, 6], F32)
        c = sb("c", [P, 64], F32)
        names = {}

        def col(name, n=1):
            k = names.setdefault(name, sum(m for m in widths.values()))
            widths.setdefault(name, n)
            return c[:, k:k + n]

        widths = {}
        mv, ve, rstd, r256 = col("mv", 2), col("ve"), col("rstd"), col("r256")
        mvD, veD, rstdD, rD = col("mvD", 2), col("veD"), col("rstdD"), col("rD")
        veR, rstdR = col("veR"), col("rstdR")
        mhalf, half = col("mhalf"), col("half")
        nt0, nt1, pre, nt2, t2 = (col(k) for k in ("nt0", "nt1", "pre", "nt2", "t2"))
        s1, s2, s3, rank, val, m8, fail, thr = (col(k) for k in ("s1", "s2", "s3", "rank", "val", "m8", "fail", "thr"))
        ndh, off, vq = col("ndh"), col("off"), col("vq")
        gs, so, ppp = col("gs"), col("so"), col("ppp")
        scale_syn, scale_out = col("scale_syn"), col("scale_out")
        fb8 = col("fb8", 8)
        failint = sb("failint", [P, 1], I32)
        pc = sb("pc", [P, 64], F32)
        rmsw = sb("rmsw", [P, KB], F32)
        syn_thr, out_thr = (pc[:, 21:22], pc[:, 22:23]), (pc[:, 46:47], pc[:, 47:48])
        bs16 = sb("bs16", [P, N // P], F32)
        halfrows = [m.bitcast(F16) for m in (pair_a, pair_b, pair_c)]
        signs_a, signs_b, signs_c = halfrows
        woutT32 = woutT.rearrange("p b n -> p (b n)").bitcast(F32)
        syn_in = [woutT32[:, 0:N], woutT32[:, N:2 * N], area1[:, 0:N], area1[:, N:2 * N]]
        out_in = [area1[:, 2 * N:3 * N], area1[:, 3 * N:4 * N], syn_in[0], syn_in[1]]
        qkv_in = area2.rearrange("p (m b d) -> p m b d", m=3, b=KB)
        syn_t = [hl[:, 0, :], hl[:, 1, :], hl[:, 0, :], unused]
        free_x, free_xn = (r[:, 3:5, :].rearrange("p a n -> p (a n)").bitcast(F16) for r in (xr, xn))
        out_t = [hl[:, 1, :], hl[:, 0, :], hl[:, 0, :], free_x]

        proj = [pb("proj0"), pb("proj1")]
        sbank = [pb("sbank0"), pb("sbank1"), pb("sbank2")]
        p_av, p_ffn, p_wo = pb("p_av"), pb("p_ffn"), pb("p_wo")
        SCORES = [1, 2, 0, 1]

        S = {k: sem(k) for k in (
            *(f"{w}_loaded{q}" for w in ("syn", "out") for q in range(4)), *(f"qkv_loaded{m}" for m in range(3)),
            *(f"{w}T{q}" for w in ("syn", "out") for q in range(4)),
            "rot_loaded", "b_loaded", "rows_loaded", "tables_loaded", "wo_loaded", "constants", "stack_zero",
            "qkv_abs", "qkv_max", "qkv_scale", "qkv_whi", "qkv_wlo", "bsyn_max", "bsyn_all", "bout_ready",
            "syn_abs", "syn_rows", "syn_sum", "syn_thr", "syn_sign", "syn_tern",
            "out_abs", "out_rows", "out_sum", "out_thr", "out_sign", "out_tern", "wo_ready", "spread", "spread_root",
            "x_loaded0", "x_loaded1", "ln_stat", "rstd_ready", "r256_ready", "xn_ready", "xh_ready", "xl_ready", "xT_ready",
            "proj_done", "qkv_out", "z_out", "rot_step", "vd_ready", "beta_added", "xnb_ready",
            "qT_done", "qTd_ready", "qk_hi", "qk_lo", "qST", "kST", "scores_done", "P_ready", "inter_done", "av_done",
            "aT_ready", "sq_ready", "kv_done", "ss_done", "veR_ready", "rstdR_ready", "wo_done", "att_added",
            "sq_sum", "kvs_ready", "stateD_ready", "state_ready",
            "guess_step", "guess_ready", "sum1", "sum2", "sum3", "nt_step", "w_out", "seg_done", "top_step",
            "fail_ready", "fail_all", "general", "thr_ready", "h_ready", "hi_ready", "lo_ready", "hiT", "loT",
            "ffn_done", "y_ready", "yst", "rstdD_ready", "yg_ready", "out_ready", "out_stored", "seed", "passed")}

        block = ctx.enter_context(nc.Block())

        class Tile:

            def __init__(self, i, k):
                self.n = i * 2 + k
                self.par = k % 2
                self.half = i + k // 2
                self.known = isinstance(i, int)

        def wait(eng, name, tile, per, n):
            value = tile.n * per + n
            if tile.known and value <= 0:
                return
            eng.wait_ge(S[name], value)

        def apart(eng):
            eng.sem_inc(S["passed"], 1)

        def slot(ring, t):
            return ring[:, bass.ds(t.n % RING, 1), :].rearrange("p a n -> p (a n)") if not t.known else ring[:, t.n % RING, :]

        def run_steps(eng, step):
            for s in range(-2, 2):
                step(eng, s // 2, s % 2)
            with eng.Fori(1, NT // 2 - 1) as i:
                step(eng, i, 0)
                step(eng, i, 1)
            for s in range(NT - 2, NT + 2):
                step(eng, s // 2, s % 2)

        def stage(i, p, k):
            t = Tile(i, p + k)
            return t if not t.known or 0 <= t.n < NT else None

        @block.sync
        def _(sp):
            ws = W_syn.rearrange("(b p) d -> p b d", p=P)
            wt = W_out.rearrange("(b p) n -> p b n", p=P)

            def rows(vector, n):
                return vector.rearrange("(a n) -> a n", a=1).broadcast_to([P, n])

            def load(dst, src, name):
                sp.dma_start(dst, src).then_inc(S[name], 16)

            def load_x(n):
                load(xr[:, n, :], x[n * P:(n + 1) * P, :], f"x_loaded{n % 2}")

            def first_loads():
                for m, W in enumerate((Wq, Wk, Wv)):
                    load(qkv_in[:, m], W.rearrange("(b p) n -> p b n", p=P), f"qkv_loaded{m}")
                load(rot, t_rot, "rot_loaded")
                load(boutx, rows(b_out, E), "b_loaded")
                load(bet, rows(beta, E), "b_loaded")
                load(bs16, b_syn.rearrange("(p a) -> p a", p=P), "b_loaded")

            def second_loads():
                for q in range(4):
                    load(syn_in[q].rearrange("p (b d) -> p b d", d=E), ws[:, 4 * q:4 * q + 4, :], f"syn_loaded{q}")
                load(gb, rows(b_syn, N), "rows_loaded")
                load(gam, rows(gamma, E), "rows_loaded")

            def third_loads():
                for dst, src in ((ident, t_ident), (qdec, t_qdec), (kdec, t_kdec), (rc, t_rc), (keep, t_keep),
                                 (iota, t_iota)):
                    load(dst, src, "tables_loaded")
                load(out_in[0], wt[:, 0, :], "out_loaded0")

            def syn_transposes():
                for q in range(4):
                    sp.wait_ge(S["syn_tern"], q + 1)
                    sp.dma_start_transpose(wsynT[:, 4 * q:4 * q + 4].rearrange("p b k t -> p (b k) t"),
                                           syn_t[q]).then_inc(S[f"synT{q}"], 16)
                    if q < 3:
                        load(out_in[q + 1], wt[:, q + 1, :], f"out_loaded{q + 1}")
                load(dmask, t_dmask, "tables_loaded")
                load(rmsw, rms_w, "wo_loaded")
                load(wo, Wo.rearrange("(b p) n -> p b n", p=P), "wo_loaded")

            def out_transposes(parts, n):
                sp.wait_ge(S["out_tern"], n)
                for q in parts:
                    sp.dma_start_transpose(woutT[:, :, q * P:(q + 1) * P], out_t[q]).then_inc(S[f"outT{q}"], 16)

            def step(sp, i, p):
                a, b, u, d = stage(i, p, 2), stage(i, p, 1), stage(i, p, -1), stage(i, p, -2)
                if a and a.known and a.n < 3:
                    if a.n == 0:
                        load_x(0)
                        load_x(1)
                        first_loads()
                elif a:
                    if a.known and a.n == 3:
                        sp.wait_ge(S["outT3"], 16)
                    wait(sp, "out_ready", a, 1, -RING + 1)
                    apart(sp)
                    sp.dma_start(slot(xr, a), x[bass.ds(a.n * P, P), :] if not a.known else x[a.n * P:(a.n + 1) * P, :]
                                 ).then_inc(S[f"x_loaded{a.par}"], 16)
                    if a.known and a.n == 3:
                        out_transposes((1,), 4)
                if u:
                    wait(sp, "hi_ready", u, 1, 1)
                    apart(sp)
                    wait(sp, "ffn_done", u, 1, 0)
                    apart(sp)
                    sp.dma_start_transpose(hT[:, 0:NB, :], hl[:, 0, :]).then_inc(S["hiT"], 16)
                if a:
                    wait(sp, "xh_ready", a, 1, 1)
                    apart(sp)
                    wait(sp, "xl_ready", a, 1, 1)
                    apart(sp)
                    wait(sp, "proj_done", a, 7, -7)
                    apart(sp)
                    sp.dma_start_transpose(xT[:, a.par], xhl.rearrange("p a n -> p (a n)")).then_inc(S["xT_ready"], 16)
                    if a.known and a.n == 0:
                        second_loads()
                    if a.known and a.n == 1:
                        load_x(2)
                        third_loads()
                if u:
                    wait(sp, "lo_ready", u, 1, 1)
                    apart(sp)
                    sp.dma_start_transpose(hT[:, NB:2 * NB, :], hl[:, 1, :]).then_inc(S["loT"], 16)
                if d:
                    wait(sp, "out_ready", d, 1, 1)
                    apart(sp)
                    sp.dma_start(out[bass.ds(d.n * P, P), :] if not d.known else out[d.n * P:(d.n + 1) * P, :], o
                                 ).then_inc(S["out_stored"], 16)

                if b:
                    if b.known and b.n == 0:
                        syn_transposes()
                    for m, name in enumerate(("qST", "kST")):
                        wait(sp, "qk_lo", b, 2, m + 1)
                        apart(sp)
                        wait(sp, "scores_done", b, 4, 0)
                        apart(sp)
                        sp.dma_start_transpose(qkst[:, m], qks[:, m].rearrange("p h a d -> p (h a d)")).then_inc(S[name], 16)
                    if b.known and b.n == 1:
                        out_transposes((0, 2, 3), 3)

            run_steps(sp, step)
            sp.wait_ge(S["out_stored"], 16 * NT)

        @block.scalar
        def _(act):
            def sums(w, parts):
                for q in parts:
                    act.wait_ge(S[f"{w}_loaded{q}"], 16)
                    n = 4 * (w == "out") + q
                    if w == "out" and q == 0:
                        act.wait_ge(S["syn_tern"], 2)
                    elif q or w == "out":
                        act.wait_ge(S[f"{w}_abs"], q)
                    else:
                        act.wait_ge(S["qkv_abs"], 3)
                    nc.scalar.activation(signs_b, (out_in if w == "out" else syn_in)[q], ACT.Abs,
                                         accum_out=pc[:, n:n + 1]).then_inc(S[f"{w}_abs"], 1)

            def signs(w, src, dst, other, thr, done):
                act.wait_ge(S[f"{w}_thr"], 1)
                nc.scalar.activation(other, src, ACT.Sign, bias=thr[1], scale=BELOW).then_inc(S[f"{w}_sign"], 1)
                if done:
                    act.wait_ge(*done)
                nc.scalar.activation(dst, src, ACT.Sign, bias=thr[0], scale=BELOW).then_inc(S[f"{w}_sign"], 1)

            def qkv_sums(m):
                act.wait_ge(S[f"qkv_loaded{m}"], 16)
                if m:
                    act.wait_ge(S["qkv_abs"], m)
                nc.scalar.activation(signs_b, qkv_in[:, m].rearrange("p b d -> p (b d)"), ACT.Abs,
                                     accum_out=pc[:, 24 + m:25 + m]).then_inc(S["qkv_abs"], 1)

            def qkv_high(m):
                act.wait_ge(S["qkv_scale"], m + 1)
                nc.scalar.activation(wqkv[:, 0, :, m * E:(m + 1) * E], qkv_in[:, m], ACT.Copy,
                                     scale=pc[:, 36 + m:37 + m]).then_inc(S["qkv_whi"], 1)

            def step(act, i, p):
                a, b, t, u = stage(i, p, 2), stage(i, p, 1), stage(i, p, 0), stage(i, p, -1)
                tile0 = t and t.known and t.n == 0

                def qkv_out(m):
                    wait(act, "proj_done", b, 7, m + 1)
                    if m == 0:
                        wait(act, "kv_done", b, 1, -1)
                        wait(act, "vd_ready", b, 1, -1)
                    dst = qk[:, b.par, m * E:(m + 1) * E] if m < 2 else v[:, b.par, :]
                    nc.scalar.activation(dst, proj[(b.par + m) % 2], ACT.Copy,
                                         scale=QS / (WS * XS)).then_inc(S["qkv_out"], 1)

                if t:
                    wait(act, "guess_ready", t, 1, 1)
                    wait(act, "z_out", t, 4, 4)
                    wait(act, "av_done", t, 4, 0)
                    if tile0:
                        act.wait_ge(S["synT3"], 16)
                    nc.scalar.activation(unused, z[:, t.par, :], ACT.Sign, bias=nt0, accum_out=s1).then_inc(S["sum1"], 1)
                    if tile0:
                        signs("out", out_in[0], out_t[0], signs_b, out_thr, (S["synT1"], 16))
                if u:
                    wait(act, "h_ready", u, 1, 1)
                    wait(act, "hiT", u, 16, 0)
                    if u.known and u.n == 0:
                        act.wait_ge(S["outT1"], 16)
                    nc.scalar.activation(hl[:, 0, :], masked, ACT.Copy).then_inc(S["hi_ready"], 1)
                if t:
                    wait(act, "state_ready", t, 1, 0)
                    if tile0:
                        act.wait_ge(S["constants"], 5)
                    for j in range(4):
                        head = slice(DH * j, DH * j + DH)
                        nc.scalar.activation(stateD[head, :, head], state[head, :].rearrange("p (g e) -> p g e", g=HG),
                                             ACT.Copy).then_inc(S["stateD_ready"], 1)
                    wait(act, "nt_step", t, 5, 2)
                    nc.scalar.activation(unused, z[:, t.par, :], ACT.Sign, bias=nt1, accum_out=s2).then_inc(S["sum2"], 1)
                if b:
                    if b.known and b.n == 0:
                        sums("syn", (0, 1))
                    qkv_out(0)
                def high_x():
                    wait(act, "xn_ready", a, 1, 1)
                    wait(act, "xT_ready", a, 16, 0)
                    nc.scalar.activation(xhl[:, 0, :], slot(xn, a), ACT.Copy).then_inc(S["xh_ready"], 1)

                if a and not (b and b.known and b.n == 0):
                    high_x()
                    if a.known and a.n == 0:
                        qkv_sums(0)
                        qkv_sums(1)
                        qkv_high(0)
                        qkv_sums(2)
                        qkv_high(1)
                        qkv_high(2)
                if tile0:
                    qkv_out(1)
                if t:
                    wait(act, "nt_step", t, 5, 5)
                    nc.scalar.activation(unused, z[:, t.par, :], ACT.Sign, bias=nt2, scale=BELOW,
                                         accum_out=s3).then_inc(S["sum3"], 1)
                if b:
                    if b.known and b.n == 0:
                        sums("syn", (2,))
                    if not tile0:
                        qkv_out(1)
                    if b.known and b.n == 0:
                        sums("syn", (3,))
                    qkv_out(2)
                    if b.known and b.n == 0:
                        high_x()
                        signs("syn", syn_in[1], syn_t[1], signs_b, syn_thr, None)
                        signs("syn", syn_in[3], syn_t[3], signs_c, syn_thr, None)
                if b:
                    for m in range(2):
                        wait(act, "rot_step", b, 4, 4)
                        wait(act, "kST" if m else "qST", b, 16, 0)
                        src = qk[:, b.par, m * E:(m + 1) * E].rearrange("p (h d) -> p h d", h=H)
                        nc.scalar.activation(qks[:, m, :, 0:2 + m:1 + m, :], src.unsqueeze(2).to_broadcast([P, H, 2, DH]),
                                             ACT.Copy).then_inc(S["qk_hi"], 1)
                    if b.known and b.n == 0:
                        sums("out", range(4))
                if t:
                    wait(act, "av_done", t, 4, 4)
                    wait(act, "wo_done", t, 1, 0)
                    nc.scalar.activation(aT.rearrange("p g c -> p (g c)"), p_av, ACT.Copy).then_inc(S["aT_ready"], 1)
                    wait(act, "ss_done", t, 1, 0)
                    nc.scalar.activation(sq.rearrange("p g c -> p (g c)"), p_av, ACT.Square).then_inc(S["sq_ready"], 1)
                if tile0:
                    signs("out", out_in[2], out_t[2], free_xn, out_thr, (S["synT2"], 16))
                    act.wait_ge(S["out_tern"], 1)
                    signs("out", out_in[3], out_t[3], signs_b, out_thr, None)

            run_steps(act, step)

        @block.gpsimd
        def _(pool):
            nc.gpsimd.memset(mhalf, -0.5).then_inc(S["constants"], 1)
            nc.gpsimd.memset(half, 0.5).then_inc(S["constants"], 1)
            nc.gpsimd.memset(ones, 1.0).then_inc(S["constants"], 1)
            nc.gpsimd.memset(state, 0.0).then_inc(S["constants"], 1)
            nc.gpsimd.memset(stateD.rearrange("p g c -> p (g c)"), 0.0).then_inc(S["constants"], 1)
            pool.wait_ge(S["constants"], 5)

            def across(dst, src, op, name):
                nc.gpsimd.partition_all_reduce(dst, src, P, op).then_inc(S[name], 1)

            def step(pool, i, p):
                a, b, t, u, d = (stage(i, p, k) for k in (2, 1, 0, -1, -2))
                if t:
                    wait(pool, "qkv_out", t, 3, 3)
                    wait(pool, "kv_done", t, 1, 0)
                    if t.known and t.n == 0:
                        pool.wait_ge(S["tables_loaded"], 7 * 16)
                        pool.wait_ge(S["syn_tern"], 4)
                    nc.gpsimd.tensor_tensor(vd.rearrange("p (h e) -> p h e", h=H),
                                            v[:, t.par, :].rearrange("p (h e) -> p h e", h=H),
                                            kdec.unsqueeze(2).to_broadcast([P, H, DH]), ALU.mult).then_inc(S["vd_ready"], 1)
                if u:
                    wait(pool, "veR_ready", u, 1, 1)
                    nc.gpsimd.tensor_tensor(rstdR, veR, mhalf, ALU.pow).then_inc(S["rstdR_ready"], 1)
                if t:
                    wait(pool, "state_ready", t, 1, 0)
                    apart(pool)
                    ch = t.n % CHUNKS
                    k = rc[:, ch, :] if t.known else rc[:, bass.ds(ch, 1), :].rearrange("p a g -> p (a g)")
                    nc.gpsimd.tensor_tensor(kvs.rearrange("p (g e) -> p g e", g=HG), state.rearrange("p (g e) -> p g e", g=HG),
                                            k.unsqueeze(2).to_broadcast([P, HG, DH]), ALU.mult).then_inc(S["kvs_ready"], 1)
                if a:
                    wait(pool, "ln_stat", a, 3, 3)
                    nc.gpsimd.tensor_tensor(rstd, ve, mhalf, ALU.pow).then_inc(S["rstd_ready"], 1)
                if u:
                    wait(pool, "hi_ready", u, 1, 1)
                    wait(pool, "loT", u, 16, 0)
                    if u.known and u.n == 0:
                        pool.wait_ge(S["outT0"], 16)
                    nc.gpsimd.tensor_tensor(hl[:, 1, :], masked, hl[:, 0, :], ALU.subtract).then_inc(S["lo_ready"], 1)
                if d:
                    wait(pool, "yst", d, 3, 3)
                    nc.gpsimd.tensor_tensor(rstdD, veD, mhalf, ALU.pow).then_inc(S["rstdD_ready"], 1)
                if a:
                    wait(pool, "xh_ready", a, 1, 1)
                    apart(pool)
                    nc.gpsimd.tensor_tensor(xhl[:, 1, :], slot(xn, a), xhl[:, 0, :], ALU.subtract).then_inc(S["xl_ready"], 1)
                    if a.known and a.n == 0:
                        for m in range(3):
                            pool.wait_ge(S["qkv_abs"], m + 1)
                            across(pc[:, 27 + m:28 + m], pc[:, 24 + m:25 + m], PMAX, "qkv_max")
                        pool.wait_ge(S["bsyn_max"], 1)
                        across(pc[:, 41:42], pc[:, 40:41], PMAX, "bsyn_all")
                        pool.wait_ge(S["qkv_wlo"], 3)
                        nc.gpsimd.memset(qks[:, :, :, 3, :], 0.0).then_inc(S["stack_zero"], 1)
                        pool.wait_ge(S["bout_ready"], 1)
                    wait(pool, "xl_ready", a, 1, 1)
                    apart(pool)
                    nc.gpsimd.tensor_tensor(slot(xn, a), slot(xn, a), boutx, ALU.add).then_inc(S["xnb_ready"], 1)
                    apart(pool)
                    nc.gpsimd.tensor_tensor(slot(xr, a), slot(xr, a), bet, ALU.add).then_inc(S["beta_added"], 1)
                if b:
                    if b.known and b.n == 0:
                        pool.wait_ge(S["syn_rows"], 1)
                        across(pc[:, 17:18], pc[:, 16:17], PADD, "syn_sum")
                        pool.wait_ge(S["rot_loaded"], 16)
                    wait(pool, "qkv_out", b, 3, 2)
                    ch = b.n % CHUNKS
                    trig = (rot[:, bass.ds(ch, 1)].rearrange("p a f e -> p (a f) e") if not b.known else rot[:, ch])
                    q4 = qk[:, b.par, :].rearrange("p (h a e) -> p h a e", a=2, e=16)
                    r4 = rt.rearrange("p (h a e) -> p h a e", a=2, e=8)
                    cos = trig[:, 0, :].unsqueeze(1).unsqueeze(1).to_broadcast([P, 2 * H, 2, 8])
                    for a_ in range(2):
                        sn = trig[:, 1 + a_, :].unsqueeze(1).to_broadcast([P, 2 * H, 8])
                        apart(pool)
                        nc.gpsimd.tensor_tensor(r4[:, :, a_], q4[:, :, 1 - a_, 0:8], sn,
                                                ALU.mult).then_inc(S["rot_step"], 1)
                    wait(pool, "rot_step", b, 4, 2)
                    apart(pool)
                    nc.gpsimd.tensor_tensor(q4[:, :, :, 0:8], q4[:, :, :, 0:8], cos, ALU.mult).then_inc(S["rot_step"], 1)
                    wait(pool, "rot_step", b, 4, 3)
                    nc.gpsimd.tensor_tensor(q4[:, :, :, 0:8], q4[:, :, :, 0:8], r4, ALU.add).then_inc(S["rot_step"], 1)
                    for m in range(2):
                        wait(pool, "qk_hi", b, 2, m + 1)
                        nc.gpsimd.tensor_tensor(qks[:, m, :, 2 - m, :],
                                                qk[:, b.par, m * E:(m + 1) * E].rearrange("p (h d) -> p h d", h=H),
                                                qks[:, m, :, 0, :], ALU.subtract).then_inc(S["qk_lo"], 1)
                    if b.known and b.n == 0:
                        pool.wait_ge(S["spread"], 1)
                        nc.gpsimd.tensor_tensor(pc[:, 55:56], pc[:, 52:53], half, ALU.pow).then_inc(S["spread_root"], 1)
                        pool.wait_ge(S["out_rows"], 1)
                        across(pc[:, 19:20], pc[:, 18:19], PADD, "out_sum")
                if t:
                    wait(pool, "sq_ready", t, 1, 1)
                    nc.gpsimd.tensor_tensor(sq[:, 0:2, :], sq[:, 0:2, :], sq[:, 2:4, :], ALU.add).then_inc(S["sq_sum"], 1)
                    wait(pool, "sq_sum", t, 2, 1)
                    nc.gpsimd.tensor_tensor(sq[:, 0, :], sq[:, 0, :], sq[:, 1, :], ALU.add).then_inc(S["sq_sum"], 1)
                    wait(pool, "fail_ready", t, 1, 1)
                    apart(pool)
                    nc.gpsimd.partition_all_reduce(failint, fail, P, PMAX).then_inc(S["fail_all"], 1)

            run_steps(pool, step)

        @block.tensor
        def _(pe):
            def step(pe, i, p):
                b, t, u, d = (stage(i, p, k) for k in (1, 0, -1, -2))

                def projection(n):
                    wait(pe, "xT_ready", b, 16, 16)
                    if n < 2:
                        wait(pe, "z_out", b, 4, n - 1)
                    elif n < 5:
                        wait(pe, "qkv_out", b, 3, n - 1)
                    else:
                        wait(pe, "z_out", b, 4, n - 4)
                    if b.known and b.n == 0:
                        if n < 3:
                            pe.wait_ge(S["qkv_wlo"], n + 1)
                        else:
                            pe.wait_ge(S[f"synT{n - 3}"], 16)
                    if n < 3:
                        pairs = [(k + KB * l, wqkv[:, w, k, n * E:(n + 1) * E]) for k in range(KB)
                                 for l, w in ((0, 0), (0, 1), (1, 0))]
                    else:
                        pairs = [(k, wsynT[:, 4 * (n - 3):4 * (n - 2), k % KB, :]) for k in range(2 * KB)]
                    bank = proj[(b.par + n) % 2]
                    for m, (k, w) in enumerate(pairs):
                        last = nc.tensor.matmul(bank, xT[:, b.par, k, :], w, start=m == 0, stop=m == len(pairs) - 1)
                    last.then_inc(S["proj_done"], 1)

                def scores(g):
                    if g == 0:
                        wait(pe, "qST", t, 16, 16)
                        wait(pe, "kST", t, 16, 16)
                        wait(pe, "P_ready", t, 4, 0)
                    elif g == 1:
                        wait(pe, "state_ready", t, 1, 0)
                    elif g == 2:
                        wait(pe, "qTd_ready", t, 1, 1)
                    else:
                        wait(pe, "P_ready", t, 4, 1)
                    for j in range(4):
                        h = 4 * g + j
                        last = nc.tensor.matmul(sbank[SCORES[g]][:, j * P:(j + 1) * P], qkst[0:96, 1, h, :],
                                                qkst[0:96, 0, h, :], start=True, stop=True)
                    last.then_inc(S["scores_done"], 1)

                def values(g):
                    wait(pe, "P_ready", t, 4, g + 1)
                    for j in range(4):
                        h = 4 * g + j
                        last = nc.tensor.matmul(p_av[32 * j:32 * j + 32, g * P:(g + 1) * P],
                                                v[:, t.par, h * DH:(h + 1) * DH], Pr[:, g % 2, j, :],
                                                start=False, stop=g == HG - 1, skip_group_check=True)
                    last.then_inc(S["av_done"], 1)

                if d:
                    wait(pe, "hiT", d, 16, 16)
                    wait(pe, "y_ready", d, 1, 0)
                    if d.known and d.n == 0:
                        for q in range(4):
                            pe.wait_ge(S[f"outT{q}"], 16)
                    for k in range(2 * NB):
                        if k == NB:
                            wait(pe, "loT", d, 16, 16)
                        last = nc.tensor.matmul(p_ffn, hT[:, k, :], woutT[:, k % NB, :], start=k == 0,
                                                stop=k == 2 * NB - 1)
                    last.then_inc(S["ffn_done"], 1)
                if t:
                    wait(pe, "rot_step", t, 4, 4)
                    if t.known and t.n == 0:
                        pe.wait_ge(S["tables_loaded"], 7 * 16)
                        pe.wait_ge(S["constants"], 5)
                    wait(pe, "veR_ready", t, 1, 0)
                    for g in range(HG):
                        last = nc.tensor.transpose(sbank[0][:, g * P:(g + 1) * P],
                                                   qk[:, t.par, g * P:(g + 1) * P], ident)
                    last.then_inc(S["qT_done"], 1)
                if b:
                    for n in range(3):
                        projection(n)
                if t:
                    wait(pe, "qTd_ready", t, 1, 1)
                    wait(pe, "stateD_ready", t, 4, 4)
                    wait(pe, "sq_ready", t, 1, 0)
                    for g in range(HG):
                        last = nc.tensor.matmul(p_av[:, g * P:(g + 1) * P], stateD[:, g, :], qTd[:, g, :],
                                                start=g == 0, stop=False, skip_group_check=True)
                    last.then_inc(S["inter_done"], 1)
                    scores(0)
                    scores(1)
                    scores(2)
                if b:
                    projection(3)
                if t:
                    scores(3)
                    values(0)
                    values(1)
                if b:
                    projection(4)
                if t:
                    values(2)
                    values(3)
                if b:
                    projection(5)
                if t:
                    wait(pe, "vd_ready", t, 1, 1)
                    wait(pe, "P_ready", t, 4, 2)
                    apart(pe)
                    for h in range(H):
                        g, j = h // 4, h % 4
                        last = nc.tensor.matmul(sbank[2][32 * j:32 * j + 32, g * DH:(g + 1) * DH],
                                                qk[:, t.par, E + h * DH:E + (h + 1) * DH],
                                                vd[:, h * DH:(h + 1) * DH], start=True, stop=True)
                    last.then_inc(S["kv_done"], 1)
                if b:
                    projection(6)
                if t:
                    wait(pe, "sq_sum", t, 2, 2)
                    wait(pe, "P_ready", t, 4, 3)
                    nc.tensor.matmul(sbank[0][:, 0:1], sq[:, 0, :], ones, start=True, stop=True).then_inc(S["ss_done"], 1)
                    wait(pe, "att_added", t, 1, 0)
                    if t.known and t.n == 0:
                        pe.wait_ge(S["wo_ready"], 1)
                    for g in range(HG):
                        last = nc.tensor.matmul(p_wo, aT[:, g, :], wo[:, g, :], start=g == 0, stop=g == HG - 1)
                    last.then_inc(S["wo_done"], 1)

            run_steps(pe, step)

        @block.vector
        def _(dve):
            done = [0]

            def then(ins):
                done[0] += 1
                ins.then_inc(S["seed"], 1)
                dve.wait_ge(S["seed"], done[0])

            def pow2(dst, src):
                then(nc.vector.tensor_scalar(dst.bitcast(I32), src.bitcast(I32), 0x7F800000, None, ALU.bitwise_and))

            def ternary(w, src, dst, scratch, thr):
                then(nc.vector.tensor_scalar(scratch, src, thr[0], 2.0, ALU.is_gt, ALU.mult))
                then(nc.vector.tensor_scalar(dst, src, thr[1], 2.0, ALU.is_lt, ALU.mult))
                nc.vector.tensor_tensor(dst, scratch, dst, ALU.subtract).then_inc(S[f"{w}_tern"], 1)

            def ternary_of_signs(w, dst, other, n):
                dve.wait_ge(S[f"{w}_sign"], n)
                nc.vector.tensor_tensor(dst, dst, other, ALU.add).then_inc(S[f"{w}_tern"], 1)

            def qkv_weights():
                for m in range(3):
                    dve.wait_ge(S["qkv_max"], m + 1)
                    then(nc.vector.tensor_scalar(pc[:, 27 + m:28 + m], pc[:, 27 + m:28 + m], 1e-30, None, ALU.max))
                    pow2(pc[:, 33 + m:34 + m], pc[:, 27 + m:28 + m])
                    then(nc.vector.reciprocal(pc[:, 36 + m:37 + m], pc[:, 33 + m:34 + m]))
                    nc.vector.tensor_scalar(pc[:, 36 + m:37 + m], pc[:, 36 + m:37 + m], WS, None,
                                            ALU.mult).then_inc(S["qkv_scale"], 1)
                    if m:
                        qkv_low(m - 1)
                qkv_low(2)
                then(nc.vector.tensor_tensor(ppp, pc[:, 33:34], pc[:, 34:35], ALU.mult))
                then(nc.vector.tensor_tensor(ppp, ppp, pc[:, 35:36], ALU.mult))
                then(nc.vector.tensor_scalar(ppp, ppp, QS ** -3, None, ALU.mult))

            def qkv_low(m):
                dve.wait_ge(S["qkv_whi"], m + 1)
                dve.wait_ge(S["qkv_scale"], m + 1)
                nc.vector.scalar_tensor_tensor(wqkv[:, 1, :, m * E:(m + 1) * E], qkv_in[:, m], pc[:, 36 + m:37 + m],
                                               wqkv[:, 0, :, m * E:(m + 1) * E], ALU.mult,
                                               ALU.subtract).then_inc(S["qkv_wlo"], 1)

            def biases():
                dve.wait_ge(S["b_loaded"], 3 * 16)
                nc.vector.tensor_scalar(boutx, boutx, XS, None, ALU.mult).then_inc(S["bout_ready"], 1)
                then(nc.vector.tensor_reduce(pc[:, 40:41], bs16, AX.X, ALU.max))
                then(nc.vector.tensor_reduce(pc[:, 42:43], bs16, AX.X, ALU.min))
                then(nc.vector.tensor_scalar(pc[:, 42:43], pc[:, 42:43], -1.0, None, ALU.mult))
                nc.vector.tensor_tensor(pc[:, 40:41], pc[:, 40:41], pc[:, 42:43], ALU.max).then_inc(S["bsyn_max"], 1)

            def mean_abs(w, c0, c1, scale, thr):
                dve.wait_ge(S[f"{w}_abs"], 4)
                nc.vector.reduce_sum(pc[:, c1:c1 + 1], pc[:, c0:c0 + 4], AX.X).then_inc(S[f"{w}_rows"], 1)
                dve.wait_ge(S[f"{w}_sum"], 1)
                then(nc.vector.tensor_scalar(scale, pc[:, c1 + 1:c1 + 2], 1.0 / (N * E), None, ALU.mult))
                then(nc.vector.tensor_scalar(thr[0], scale, 1e-8, 0.5, ALU.add, ALU.mult))
                nc.vector.tensor_scalar(thr[1], thr[0], -1.0, None, ALU.mult).then_inc(S[f"{w}_thr"], 1)
                dve.wait_ge(S[f"{w}_thr"], 1)

            def syn_weights():
                mean_abs("syn", 0, 16, scale_syn, syn_thr)
                ternary("syn", syn_in[0], syn_t[0], signs_a, syn_thr)
                dve.wait_ge(S["rows_loaded"], 2 * 16)
                dve.wait_ge(S["bsyn_all"], 1)
                then(nc.vector.scalar_tensor_tensor(pc[:, 42:43], scale_syn, float(E), pc[:, 41:42], ALU.mult, ALU.add))
                then(nc.vector.tensor_scalar(pc[:, 42:43], pc[:, 42:43], 1e-30, None, ALU.max))
                pow2(pc[:, 43:44], pc[:, 42:43])
                then(nc.vector.reciprocal(pc[:, 44:45], pc[:, 43:44]))
                then(nc.vector.tensor_scalar(pc[:, 44:45], pc[:, 44:45], 16384.0, None, ALU.mult))
                then(nc.vector.scalar_tensor_tensor(gs, scale_syn, 0.5 / XS, pc[:, 44:45], ALU.mult, ALU.mult))
                ternary_of_signs("syn", syn_t[1], signs_b, 2)
                then(nc.vector.tensor_scalar(gb, gb, pc[:, 44:45], None, ALU.mult))
                dve.wait_ge(S["synT0"], 16)
                ternary("syn", syn_in[2], syn_t[2], signs_a, syn_thr)
                ternary_of_signs("syn", syn_t[3], signs_c, 4)

            def step(dve, i, p):
                a, b, t, u, d = (stage(i, p, k) for k in (2, 1, 0, -1, -2))

                def probs(g):
                    wait(dve, "scores_done", t, 4, g + 1)
                    wait(dve, "av_done", t, 4, g - 1)
                    wait(dve, "sum3", t, 1, 1)
                    nc.vector.scalar_tensor_tensor(Pr[:, g % 2].rearrange("p j c -> p (j c)"), sbank[SCORES[g]], ppp,
                                                   dmask[:, 4 * g:4 * g + 4, :].rearrange("p j c -> p (j c)"),
                                                   ALU.mult, ALU.mult).then_inc(S["P_ready"], 1)

                def z_chunk(n):
                    wait(dve, "proj_done", b, 7, 4 + n)
                    if n == 0:
                        wait(dve, "h_ready", b, 1, -1)
                    nc.vector.scalar_tensor_tensor(z[:, b.par, n * 512:(n + 1) * 512], proj[(b.par + 3 + n) % 2], gs,
                                                   gb[:, n * 512:(n + 1) * 512], ALU.mult, ALU.add).then_inc(S["z_out"], 1)
                    if b.known and b.n == 0:
                        wait(dve, "z_out", b, 4, n + 1)
                        then(nc.vector.bn_stats(seed6[:, n, :], z[:, 0, n * 512:(n + 1) * 512]))

                def segments(k):
                    wait(dve, "w_out", t, 1, 1)
                    wait(dve, "top_step", t, 12, 0)
                    for n in range(4 * k, 4 * k + 4):
                        apart(dve)
                        nc.vector.max(cand[:, 0, 8 * n:8 * n + 8], masked[:, n * SEG:(n + 1) * SEG]).then_inc(S["seg_done"], 1)

                if u:
                    wait(dve, "kv_done", u, 1, 1)
                    wait(dve, "kvs_ready", u, 1, 1)
                    ch = u.n % CHUNKS
                    kp = keep[:, bass.ds(ch, 1)] if not u.known else keep[:, ch:ch + 1]
                    nc.vector.scalar_tensor_tensor(state, sbank[2][:, 0:P], kp, kvs, ALU.mult, ALU.add).then_inc(S["state_ready"], 1)
                    wait(dve, "ss_done", u, 1, 1)
                    nc.vector.tensor_scalar(veR, sbank[0][:, 0:1], 1.0 / E, LN_EPS, ALU.mult, ALU.add).then_inc(S["veR_ready"], 1)
                    wait(dve, "fail_all", u, 1, 1)
                    apart(dve)
                    missed = dve.value_load(failint[0:1, 0:1])
                    with dve.If(missed > 0):
                        wait(dve, "seg_done", u, 16, 16)
                        nc.vector.tensor_copy(masked, z[:, u.par, :]).then_inc(S["general"], 1)
                        with dve.Fori(0, TOPK // 8) as r:
                            dve.wait_ge(S["general"], u.n * FB + r * 2 + 1)
                            apart(dve)
                            nc.vector.max(fb8, masked).then_inc(S["general"], 1)
                            dve.wait_ge(S["general"], u.n * FB + r * 2 + 2)
                            apart(dve)
                            nc.vector.match_replace(masked, fb8, masked, -BIG).then_inc(S["general"], 1)
                        dve.wait_ge(S["general"], u.n * FB + FB - 2)
                        apart(dve)
                        nc.vector.max(fb8, masked).then_inc(S["general"], 1)
                        dve.wait_ge(S["general"], u.n * FB + FB - 1)
                        nc.vector.tensor_copy(val, fb8[:, TOPK % 8 - 1:TOPK % 8]).then_inc(S["general"], 1)
                    with dve.Else():
                        dve.sem_inc(S["general"], FB)
                    dve.wait_ge(S["general"], u.n * FB + FB)
                    nc.vector.tensor_scalar(thr, val, 0.0, None, ALU.max).then_inc(S["thr_ready"], 1)
                    nc.vector.tensor_scalar(vq, val, -0.25, None, ALU.mult).then_inc(S["guess_step"], 1)
                    wait(dve, "guess_step", u, 1, 1)
                    nc.vector.scalar_tensor_tensor(nt0, nt0, 0.75, vq, ALU.mult, ALU.add).then_inc(S["guess_ready"], 1)
                    wait(dve, "thr_ready", u, 1, 1)
                    nc.vector.scalar_tensor_tensor(masked, z[:, u.par, :], thr, z[:, u.par, :], ALU.is_ge,
                                                   ALU.mult).then_inc(S["h_ready"], 1)
                if a:
                    dve.wait_ge(S[f"x_loaded{a.par}"], a.half * 16 + 16)
                    nc.vector.bn_stats(st6[:, 0, :], slot(xr, a)).then_inc(S["ln_stat"], 1)
                    wait(dve, "ln_stat", a, 3, 1)
                    apart(dve)
                    nc.vector.bn_aggr(mv, st6[:, 0:1, :]).then_inc(S["ln_stat"], 1)
                    wait(dve, "ln_stat", a, 3, 2)
                    nc.vector.tensor_scalar(ve, mv[:, 1:2], LN_EPS, None, ALU.add).then_inc(S["ln_stat"], 1)
                if t and t.known and t.n == 0:
                    then(nc.vector.bn_aggr(pc[:, 50:52], seed6))
                    nc.vector.tensor_scalar(pc[:, 52:53], pc[:, 51:52], 1e-30, None, ALU.max).then_inc(S["spread"], 1)
                    dve.wait_ge(S["spread_root"], 1)
                    then(nc.vector.tensor_scalar(ndh, pc[:, 55:56], -0.5 / 359.4, None, ALU.mult))
                    then(nc.vector.tensor_scalar(off, pc[:, 55:56], 0.5 / 359.4 * (N - 2 * (TOPK - AIM)), None, ALU.mult))
                    then(nc.vector.tensor_scalar(pc[:, 56:57], pc[:, 50:51], -1.0, None, ALU.mult))
                    nc.vector.scalar_tensor_tensor(nt0, pc[:, 55:56], -1.2816, pc[:, 56:57], ALU.mult,
                                                   ALU.add).then_inc(S["guess_ready"], 1)
                    mean_abs("out", 4, 18, scale_out, out_thr)
                    then(nc.vector.scalar_tensor_tensor(so, scale_out, 0.5 * XS / 16384.0, pc[:, 43:44], ALU.mult, ALU.mult))
                    dve.wait_ge(S["tables_loaded"], 7 * 16)
                if u:
                    wait(dve, "wo_done", u, 1, 1)
                    wait(dve, "rstdR_ready", u, 1, 1)
                    wait(dve, "beta_added", u, 1, 1)
                    nc.vector.scalar_tensor_tensor(slot(xr, u), p_wo, rstdR, slot(xr, u), ALU.mult,
                                                   ALU.add).then_inc(S["att_added"], 1)
                if t:
                    wait(dve, "guess_ready", t, 1, 1)
                    nc.vector.tensor_scalar(pre, nt0, off, None, ALU.subtract).then_inc(S["nt_step"], 1)
                    wait(dve, "sum1", t, 1, 1)
                    wait(dve, "nt_step", t, 5, 1)
                    nc.vector.tensor_scalar(nt1, s1, ndh, pre, ALU.mult, ALU.add).then_inc(S["nt_step"], 1)
                if a:
                    wait(dve, "rstd_ready", a, 1, 1)
                    nc.vector.tensor_scalar(r256, rstd, XS, None, ALU.mult).then_inc(S["r256_ready"], 1)
                    wait(dve, "r256_ready", a, 1, 1)
                    if a.known and a.n == 3:
                        dve.wait_ge(S["out_tern"], 4)
                    nc.vector.tensor_scalar(slot(xn, a), slot(xr, a), mv[:, 0:1], r256, ALU.subtract,
                                            ALU.mult).then_inc(S["xn_ready"], 1)
                    if a.known and a.n == 0:
                        qkv_weights()
                        biases()
                if t:
                    wait(dve, "qT_done", t, 1, 1)
                    nc.vector.scalar_tensor_tensor(qTd.rearrange("p g c -> p (g c)"), sbank[0], ppp,
                                                   qdec.rearrange("p g c -> p (g c)"), ALU.mult,
                                                   ALU.mult).then_inc(S["qTd_ready"], 1)
                    wait(dve, "nt_step", t, 5, 2)
                    nc.vector.tensor_scalar(pre, nt1, off, None, ALU.subtract).then_inc(S["nt_step"], 1)
                    wait(dve, "sum2", t, 1, 1)
                    wait(dve, "nt_step", t, 5, 3)
                    nc.vector.tensor_scalar(nt2, s2, ndh, pre, ALU.mult, ALU.add).then_inc(S["nt_step"], 1)
                    wait(dve, "nt_step", t, 5, 4)
                    nc.vector.tensor_scalar(t2, nt2, -1.0, None, ALU.mult).then_inc(S["nt_step"], 1)
                if d:
                    wait(dve, "ffn_done", d, 1, 1)
                    wait(dve, "xnb_ready", d, 1, 1)
                    wait(dve, "out_ready", d, 1, 0)
                    if d.known and d.n == 0:
                        dve.wait_ge(S["out_tern"], 4)
                    nc.vector.scalar_tensor_tensor(y, p_ffn, so, slot(xn, d), ALU.mult, ALU.add).then_inc(S["y_ready"], 1)
                    wait(dve, "y_ready", d, 1, 1)
                    nc.vector.bn_stats(st6[:, 1, :], y).then_inc(S["yst"], 1)
                    wait(dve, "yst", d, 3, 1)
                    apart(dve)
                    nc.vector.bn_aggr(mvD, st6[:, 1:2, :]).then_inc(S["yst"], 1)
                    wait(dve, "yst", d, 3, 2)
                    nc.vector.tensor_scalar(veD, mvD[:, 1:2], 1.0 / (XS * XS), LN_EPS, ALU.mult, ALU.add).then_inc(S["yst"], 1)
                    nc.vector.scalar_tensor_tensor(y, y, mvD[:, 0:1], gam, ALU.subtract, ALU.mult).then_inc(S["yg_ready"], 1)
                    wait(dve, "rstdD_ready", d, 1, 1)
                    nc.vector.tensor_scalar(rD, rstdD, 1.0 / XS, None, ALU.mult).then_inc(S["yg_ready"], 1)
                    wait(dve, "yg_ready", d, 2, 2)
                    wait(dve, "out_stored", d, 16, 0)
                    wait(dve, "att_added", d, 1, 1)
                    nc.vector.scalar_tensor_tensor(o, y, rD, slot(xr, d), ALU.mult, ALU.add).then_inc(S["out_ready"], 1)
                def below():
                    wait(dve, "nt_step", t, 5, 5)
                    wait(dve, "lo_ready", t, 1, 0)
                    nc.vector.scalar_tensor_tensor(masked, z[:, t.par, :], t2, z[:, t.par, :], ALU.is_le,
                                                   ALU.mult).then_inc(S["w_out"], 1)

                tile0 = t and t.known and t.n == 0
                if t and not tile0:
                    below()
                if t:
                    probs(0)
                    probs(1)
                    if not tile0:
                        segments(0)
                if b:
                    if b.known and b.n == 0:
                        syn_weights()
                    z_chunk(0)
                if t:
                    probs(2)
                    probs(3)
                    if tile0:
                        ternary_of_signs("out", out_t[0], signs_b, 2)
                        below()
                        segments(0)
                    segments(1)
                if b:
                    z_chunk(1)
                if t:
                    segments(2)
                if b:
                    z_chunk(2)
                if t:
                    segments(3)
                if tile0:
                    dve.wait_ge(S["wo_loaded"], 2 * 16)
                    for k in range(KB):
                        last = nc.vector.tensor_scalar(wo[:, k, :], wo[:, k, :], rmsw[:, k:k + 1], None, ALU.mult)
                    last.then_inc(S["wo_ready"], 1)
                    ternary_of_signs("out", out_t[2], free_xn, 4)
                if b:
                    z_chunk(3)
                if t:
                    wait(dve, "sum3", t, 1, 1)
                    nc.vector.tensor_scalar(rank, s3, -0.5, TOPK - N / 2, ALU.mult, ALU.add).then_inc(S["top_step"], 1)
                    wait(dve, "seg_done", t, 16, 16)
                    nc.vector.tensor_reduce(m8, cand[:, 0, :].rearrange("p (s k) -> p s k", k=8)[:, :, 7], AX.X,
                                            ALU.max).then_inc(S["top_step"], 1)
                    for r in range(RANKS // 8):
                        apart(dve)
                        nc.vector.max(top[:, 8 * r:8 * r + 8], cand[:, r % 2, :]).then_inc(S["top_step"], 1)
                        if r < RANKS // 8 - 1:
                            wait(dve, "top_step", t, 12, 3 + 2 * r)
                            apart(dve)
                            nc.vector.match_replace(cand[:, (r + 1) % 2, :], top[:, 8 * r:8 * r + 8], cand[:, r % 2, :],
                                                    -BIG).then_inc(S["top_step"], 1)
                            wait(dve, "top_step", t, 12, 4 + 2 * r)
                    wait(dve, "top_step", t, 12, 9)
                    nc.vector.scalar_tensor_tensor(sel, iota, rank, top, ALU.is_equal, ALU.mult,
                                                   accum_out=val).then_inc(S["top_step"], 1)
                    wait(dve, "top_step", t, 12, 10)
                    nc.vector.tensor_scalar(pre, val, 0.0, None, ALU.is_le).then_inc(S["top_step"], 1)
                    nc.vector.tensor_tensor(s1, m8, val, ALU.is_gt).then_inc(S["top_step"], 1)
                    wait(dve, "top_step", t, 12, 12)
                    nc.vector.tensor_tensor(fail, pre, s1, ALU.max).then_inc(S["fail_ready"], 1)
                    if t.known and t.n == 0:
                        ternary_of_signs("out", out_t[3], signs_b, 6)
                        dve.wait_ge(S["outT2"], 16)
                        ternary("out", out_in[1], out_t[1], free_xn, out_thr)

            run_steps(dve, step)


_INS = ["L0_attn_x", "L0_attn_Wq", "L0_attn_Wk", "L0_attn_Wv", "L0_attn_Wo", "L0_attn_rms_w", "L0_ffn_W_syn",
        "L0_ffn_b_syn", "L0_ffn_W_out", "L0_ffn_b_out", "L0_ffn_gamma", "L0_ffn_beta"]


def tables():
    import numpy as np

    f = np.float32
    freq = (f(1.0 / 1024.0) ** np.linspace(0.0, 1.0, DH // 4, dtype=f)).astype(f)
    theta = (np.arange(CHUNKS * P, dtype=f)[:, None] * freq[None, :]).astype(f).astype(np.float64)
    cos, sin = np.cos(theta), np.sin(theta)
    rot = np.stack([cos, sin, -sin], 1).reshape(CHUNKS, P, 3, 8).transpose(1, 0, 2, 3)
    start = 2.0 ** (-2.0 ** (-(np.log2(H) - 3)))
    slopes = np.array([start * start ** i for i in range(H)]).astype(f)
    r = np.exp(-slopes.astype(np.float64)).astype(f).astype(np.float64)
    i = np.arange(P)
    diff = i[None, :] - i[:, None]
    dmask = np.where(diff[:, None, :] >= 0, r[None, :, None] ** np.maximum(diff, 0)[:, None, :], 0.0)
    rg = r.reshape(HG, 4)
    qdec = np.repeat(rg.T, DH, axis=0)[:, :, None] ** (i[None, None, :] + 1.0)
    kdec = r[None, :] ** (127.0 - i[:, None])
    keep = np.tile((np.arange(CHUNKS) < CHUNKS - 1).astype(f), (P, 1))
    rc = keep[:, :, None] * np.repeat(rg.T ** 128.0, DH, axis=0)[:, None, :]
    iota = np.tile(np.arange(1, RANKS + 1, dtype=f), (P, 1))
    return {k: np.ascontiguousarray(a, dtype=f) for k, a in dict(
        t_rot=rot, t_dmask=dmask, t_qdec=qdec, t_kdec=kdec, t_rc=rc, t_keep=keep, t_ident=np.eye(P),
        t_iota=iota).items()}


def kernel(**inputs):
    import numpy as _np
    import concourse.bacc as _bacc
    from concourse import mybir as _mybir
    from concourse.bass_utils import run_bass_kernel_spmd as _run

    nc = _bacc.Bacc("TRN2", target_bir_lowering=False, num_devices=1)
    arrays, args = {}, []
    for name in _INS:
        a = _np.ascontiguousarray(inputs[name])
        if name == "L0_attn_x":
            a = a.reshape(NT * P, E)
        if name == "L0_attn_rms_w":
            a = _np.ascontiguousarray(a.reshape(KB, P).T)
        arrays[f"in_{name}_dram"] = a
        args.append(nc.dram_tensor(f"in_{name}_dram", a.shape, _mybir.dt.from_np(a.dtype), kind="ExternalInput").ap())
    for name, a in tables().items():
        arrays[f"{name}_dram"] = a
        args.append(nc.dram_tensor(f"{name}_dram", a.shape, _mybir.dt.from_np(a.dtype), kind="ExternalInput").ap())
    args.append(nc.dram_tensor("out_0_dram", (NT * P, E), F32, kind="ExternalOutput").ap())
    build(nc, *args)
    r = _run(nc, [arrays], core_ids=[0])
    return r.results[0]["out_0_dram"].reshape(4, NT * P // 4, E)
```

```python
from contextlib import ExitStack

import concourse.bass as bass
from concourse import mybir

F32 = mybir.dt.float32
F16 = mybir.dt.float16
BF16 = mybir.dt.bfloat16
I32 = mybir.dt.int32
ALU = mybir.AluOpType
ACT = mybir.ActivationFunctionType
AX = mybir.AxisListType
PMAX = bass.bass_isa.ReduceOp.max
PADD = bass.bass_isa.ReduceOp.add

P = 128
E = 512
H, DH = 16, 32
HG = H // 4
N = 2048
KB = E // P
NB = N // P
TOPK = max(1, int(N * (1.0 - 0.9)))
NT = 32
CHUNKS = 8
RING = 5
AS = 256.0
XS = 256.0
WS = 2.0 ** 14
QS = 32.0
LN_EPS = 1e-5
RANKS = 32
AIM = 19.5
SEGS = 16
SEG = N // SEGS
BIG = 3.0e38
BELOW = 1.0 - 2.0 ** -24
FB = 3 + 2 * (TOPK // 8)
assert TOPK % 8 != 0


def build(nc, x, Wq, Wk, Wv, Wo, rms_w, W_syn, b_syn, W_out, b_out, gamma, beta,
          t_rot, t_dmask, t_qdec, t_kdec, t_rc, t_keep, t_ident, t_iota, out):
    ctx = ExitStack()
    with ctx:
        def sb(name, shape, dt):
            return ctx.enter_context(nc.sbuf_tensor(name, shape, dt))[:]

        def pb(name):
            return ctx.enter_context(nc.psum_tensor(name, [P, 512], F32))[:]

        def sem(name):
            return ctx.enter_context(nc.semaphore(name))

        wqkv = sb("wqkv", [P, 2, KB, 3 * E], F16)
        wsynT = sb("wsynT", [P, NB, KB, P], F16)
        woutT = sb("woutT", [P, NB, E], F16)
        wo = sb("wo", [P, 2, KB, E], F16)
        rot = sb("rot", [P, CHUNKS, 3, 8], F32)
        dmask = sb("dmask", [P, H, P], F32)
        qdec = sb("qdec", [P, HG, P], F32)
        kdec = sb("kdec", [P, H], F32)
        rc = sb("rc", [P, CHUNKS, HG], F32)
        keep = sb("keep", [P, CHUNKS], F32)
        ident = sb("ident", [P, P], F32)
        iota = sb("iota", [P, RANKS], F32)
        ones = sb("ones", [P, P], F32)
        gb = sb("gb", [P, N], F32)
        boutx = sb("boutx", [P, E], F32)
        gam = sb("gam", [P, E], F32)
        bet = sb("bet", [P, E], F32)
        area1 = sb("area1", [P, 4 * N], F32)
        z = area1[:, 0:2 * N].rearrange("p (r n) -> p r n", r=2)
        masked = area1[:, 2 * N:3 * N]
        hT = area1[:, 3 * N:4 * N].bitcast(F16).rearrange("p (b t) -> p b t", t=P)
        area2 = sb("area2", [P, 3 * KB * E], F32)
        qks = area2[:, 2048:4096].bitcast(F16).rearrange("p (m h a d) -> p m h a d", m=2, h=H, a=4)
        qkst = area2[:, 4096:6144].bitcast(F16).rearrange("p (m h c) -> p m h c", m=2, h=H)
        qk = area2[:, 0:2048].rearrange("p (r n) -> p r n", r=2)
        v = sb("v", [P, 2, E], F32)
        Pr = sb("Pr", [P, 2, 4, P], F32)
        unused = Pr.rearrange("p r j c -> p (r j c)").bitcast(F16)
        pair_c = sb("pair_c", [P, 2 * E], F32)
        qTd = pair_c[:, 0:E].rearrange("p (g c) -> p g c", g=HG)
        rt = pair_c[:, 0:E]
        vd = pair_c[:, E:2 * E]
        hl = sb("hl", [P, 2, N], F16)
        xr = sb("xr", [P, RING, E], F32)
        xn = sb("xn", [P, RING, E], F32)
        xhl = sb("xhl", [P, 2, E], F16)
        xT = sb("xT", [P, 2, 2 * KB, P], F16)
        pair_a = sb("pair_a", [P, 2 * E], F32)
        aT = pair_a[:, 0:E].rearrange("p (g c) -> p g c", g=HG)
        sq = pair_a[:, E:2 * E].rearrange("p (g c) -> p g c", g=HG)
        rdiag = sq[:, 3, :]
        ahl = sb("ahl", [P, 2, HG, P], F16)
        state = sb("state", [P, P], F32)
        stateD = sb("stateD", [P, HG, P], F32)
        kvs = sb("kvs", [P, P], F32)
        pair_b = sb("pair_b", [P, 2 * E], F32)
        y, o = pair_b[:, 0:E], pair_b[:, E:2 * E]
        cand = sb("cand", [P, 2, SEGS * 8], F32)
        top = sb("top", [P, RANKS], F32)
        sel = sb("sel", [P, RANKS], F32)
        st6 = sb("st6", [P, 2, 6], F32)
        seed6 = sb("seed6", [P, 4, 6], F32)
        c = sb("c", [P, 64], F32)
        names = {}

        def col(name, n=1):
            k = names.setdefault(name, sum(m for m in widths.values()))
            widths.setdefault(name, n)
            return c[:, k:k + n]

        widths = {}
        mv, ve, rstd, r256 = col("mv", 2), col("ve"), col("rstd"), col("r256")
        mvD, veD, rstdD, rD = col("mvD", 2), col("veD"), col("rstdD"), col("rD")
        mrD = col("mrD")
        veR, rstdR, wos = col("veR"), col("rstdR"), col("wos")
        mhalf, half = col("mhalf"), col("half")
        nt0, nt1, pre, nt2, t2 = (col(k) for k in ("nt0", "nt1", "pre", "nt2", "t2"))
        s1, s2, s3, rank, val, m8, fail, thr = (col(k) for k in ("s1", "s2", "s3", "rank", "val", "m8", "fail", "thr"))
        ndh, off, vq = col("ndh"), col("off"), col("vq")
        gs, so, ppp = col("gs"), col("so"), col("ppp")
        scale_syn, scale_out = col("scale_syn"), col("scale_out")
        fb8 = col("fb8", 8)
        failint = sb("failint", [P, 1], I32)
        pc = sb("pc", [P, 64], F32)
        rmsw = sb("rmsw", [P, KB], F32)
        syn_thr, out_thr = (pc[:, 21:22], pc[:, 22:23]), (pc[:, 46:47], pc[:, 47:48])
        bs16 = sb("bs16", [P, N // P], F32)
        wo_in = area1[:, 2 * N:3 * N].rearrange("p (b n) -> p b n", b=KB)
        halfrows = [m.bitcast(F16) for m in (pair_a, pair_b, pair_c)]
        signs_a, signs_b, signs_c = halfrows
        woutT32 = woutT.rearrange("p b n -> p (b n)").bitcast(F32)
        syn_in = [woutT32[:, 0:N], woutT32[:, N:2 * N], area1[:, 0:N], area1[:, N:2 * N]]
        out_in = [area1[:, 3 * N:4 * N], area1[:, 3 * N:4 * N], syn_in[0], syn_in[1]]
        qkv_in = area2.rearrange("p (m b d) -> p m b d", m=3, b=KB)
        free_x, free_xn = (r[:, 3:5, :].rearrange("p a n -> p (a n)").bitcast(F16) for r in (xr, xn))
        syn_t = [hl[:, 0, :], hl[:, 1, :], free_x, unused]
        out_t = [signs_a, hl[:, 1, :], hl[:, 0, :], free_xn]

        proj = [pb("proj0"), pb("proj1")]
        sbank = [pb("sbank0"), pb("sbank1"), pb("sbank2")]
        p_av, p_ffn, p_wo = pb("p_av"), pb("p_ffn"), pb("p_wo")
        SCORES = [1, 2, 0, 1]

        S = {k: sem(k) for k in (
            *(f"{w}_loaded{q}" for w in ("syn", "out") for q in range(4)), *(f"qkv_loaded{m}" for m in range(3)),
            *(f"{w}T{q}" for w in ("syn", "out") for q in range(4)),
            "rot_loaded", "b_loaded", "rows_loaded", "tables_loaded", "dmask_loaded", "wo_loaded", "constants", "stack_zero",
            "qkv_abs", "qkv_max", "qkv_scale", "qkv_whi", "qkv_wlo", "bsyn_max", "bsyn_all", "bout_ready",
            "syn_abs", "syn_rows", "syn_sum", "syn_thr", "syn_sign", "syn_tern",
            "out_abs", "out_rows", "out_sum", "out_thr", "out_sign", "out_tern", "wo_scaled", "wo_abs", "wo_max", "wo_scale", "wo_hi", "wo_ready", "spread", "spread_root",
            "x_loaded0", "x_loaded1", "ln_stat", "rstd_ready", "r256_ready", "xn_ready", "xh_ready", "xl_ready", "xT_ready",
            "qkv_done", "z_done", "qkv_out", "z_out", "rot_step", "vd_ready", "beta_added", "xnb_ready",
            "qT_done", "qTd_ready", "qk_hi", "qk_lo", "qST", "kST", "scores_done", "P_ready", "inter_done", "av_done",
            "aT_ready", "an_ready", "ah_ready", "al_ready", "sq_ready", "kv_done", "ss_done", "veR_ready", "rstdR_ready", "rdiag_ready", "rall_done", "wo_done", "att_added",
            "sq_sum", "kvs_ready", "stateD_ready", "state_ready",
            "guess_step", "guess_ready", "sum1", "sum2", "sum3", "nt_step", "w_out", "seg_done", "top_step",
            "fail_ready", "fail_all", "general", "thr_ready", "h_ready", "hi_ready", "lo_ready", "hiT", "loT",
            "ffn_done", "y_ready", "yst", "rstdD_ready", "yn_ready", "yg_ready", "out_ready", "out_stored", "seed", "passed")}

        block = ctx.enter_context(nc.Block())

        class Tile:

            def __init__(self, i, k):
                self.n = i * 2 + k
                self.par = k % 2
                self.half = i + k // 2
                self.known = isinstance(i, int)

        def wait(eng, name, tile, per, n):
            value = tile.n * per + n
            if tile.known and value <= 0:
                return
            eng.wait_ge(S[name], value)

        def apart(eng):
            eng.sem_inc(S["passed"], 1)

        def slot(ring, t):
            return ring[:, bass.ds(t.n % RING, 1), :].rearrange("p a n -> p (a n)") if not t.known else ring[:, t.n % RING, :]

        def run_steps(eng, step):
            for s in range(-2, 2):
                step(eng, s // 2, s % 2)
            with eng.Fori(1, NT // 2 - 1) as i:
                step(eng, i, 0)
                step(eng, i, 1)
            for s in range(NT - 2, NT + 2):
                step(eng, s // 2, s % 2)

        def stage(i, p, k):
            t = Tile(i, p + k)
            return t if not t.known or 0 <= t.n < NT else None

        @block.sync
        def _(sp):
            ws = W_syn.rearrange("(b p) d -> p b d", p=P)
            wt = W_out.rearrange("(b p) n -> p b n", p=P)

            def rows(vector, n):
                return vector.rearrange("(a n) -> a n", a=1).broadcast_to([P, n])

            def load(dst, src, name):
                sp.dma_start(dst, src).then_inc(S[name], 16)

            def load_x(n):
                load(xr[:, n, :], x[n * P:(n + 1) * P, :], f"x_loaded{n % 2}")

            def first_loads():
                for m, W in enumerate((Wq, Wk, Wv)):
                    load(qkv_in[:, m], W.rearrange("(b p) n -> p b n", p=P), f"qkv_loaded{m}")
                load(rot, t_rot, "rot_loaded")
                load(boutx, rows(b_out, E), "b_loaded")
                load(bet, rows(beta, E), "b_loaded")
                load(bs16, b_syn.rearrange("(p a) -> p a", p=P), "b_loaded")

            def second_loads():
                for q in range(4):
                    load(syn_in[q].rearrange("p (b d) -> p b d", d=E), ws[:, 4 * q:4 * q + 4, :], f"syn_loaded{q}")

            def third_loads():
                load(gb, rows(b_syn, N), "rows_loaded")
                load(gam, rows(gamma, E), "rows_loaded")
                for dst, src in ((ident, t_ident), (qdec, t_qdec), (kdec, t_kdec), (rc, t_rc), (keep, t_keep),
                                 (iota, t_iota)):
                    load(dst, src, "tables_loaded")
                load(rmsw, rms_w, "wo_loaded")
                load(wo_in, Wo.rearrange("(b p) n -> p b n", p=P), "wo_loaded")

            def syn_transposes():
                for q in range(4):
                    sp.wait_ge(S["syn_tern"], q + 1)
                    sp.dma_start_transpose(wsynT[:, 4 * q:4 * q + 4].rearrange("p b k t -> p (b k) t"),
                                           syn_t[q]).then_inc(S[f"synT{q}"], 16)
                    if q == 1:
                        load(out_in[0], wt[:, 0, :], "out_loaded0")

            def fourth_loads():
                load(dmask, t_dmask, "dmask_loaded")
                for q in range(2, 4):
                    load(out_in[q], wt[:, q, :], f"out_loaded{q}")
                sp.wait_ge(S["out_abs"], 1)
                load(out_in[1], wt[:, 1, :], "out_loaded1")

            def out_transpose(q, n):
                sp.wait_ge(S["out_tern"], n)
                sp.dma_start_transpose(woutT[:, :, q * P:(q + 1) * P], out_t[q]).then_inc(S[f"outT{q}"], 16)

            def step(sp, i, p):
                a, b, u, d = stage(i, p, 2), stage(i, p, 1), stage(i, p, -1), stage(i, p, -2)
                if a and a.known and a.n < 4:
                    if a.n == 0:
                        load_x(0)
                        load_x(1)
                        first_loads()
                elif a:
                    wait(sp, "out_ready", a, 1, -RING + 1)
                    apart(sp)
                    sp.dma_start(slot(xr, a), x[bass.ds(a.n * P, P), :] if not a.known else x[a.n * P:(a.n + 1) * P, :]
                                 ).then_inc(S[f"x_loaded{a.par}"], 16)
                def high_transposes():
                    wait(sp, "hi_ready", u, 1, 1)
                    apart(sp)
                    wait(sp, "ffn_done", u, 1, 0)
                    apart(sp)
                    sp.dma_start_transpose(hT[:, 0:NB, :], hl[:, 0, :]).then_inc(S["hiT"], 16)

                if u and not (u.known and u.n == 0):
                    high_transposes()
                if a:
                    wait(sp, "xh_ready", a, 1, 1)
                    apart(sp)
                    wait(sp, "xl_ready", a, 1, 1)
                    apart(sp)
                    wait(sp, "z_done", a, 4, -4)
                    apart(sp)
                    sp.dma_start_transpose(xT[:, a.par], xhl.rearrange("p a n -> p (a n)")).then_inc(S["xT_ready"], 16)
                    if a.known and a.n == 0:
                        second_loads()
                    if a.known and a.n == 1:
                        load_x(2)
                        third_loads()
                    if a.known and a.n == 2:
                        sp.wait_ge(S["synT2"], 16)
                        load_x(3)
                if u and u.known and u.n == 0:
                    out_transpose(0, 4)
                    high_transposes()
                if u:
                    wait(sp, "lo_ready", u, 1, 1)
                    apart(sp)
                    sp.dma_start_transpose(hT[:, NB:2 * NB, :], hl[:, 1, :]).then_inc(S["loT"], 16)
                if b:
                    if b.known and b.n == 0:
                        syn_transposes()
                    for m, name in enumerate(("qST", "kST")):
                        wait(sp, "qk_lo", b, 2, m + 1)
                        apart(sp)
                        wait(sp, "scores_done", b, 4, 0)
                        apart(sp)
                        sp.dma_start_transpose(qkst[:, m], qks[:, m].rearrange("p h a d -> p (h a d)")).then_inc(S[name], 16)
                    if b.known and b.n == 0:
                        fourth_loads()
                    if b.known and b.n == 1:
                        out_transpose(2, 2)
                        out_transpose(3, 2)
                        out_transpose(1, 3)
                        load(out_in[0], wt[:, 0, :], "out_loaded0")
                if d:
                    wait(sp, "out_ready", d, 1, 1)
                    apart(sp)
                    sp.dma_start(out[bass.ds(d.n * P, P), :] if not d.known else out[d.n * P:(d.n + 1) * P, :], o
                                 ).then_inc(S["out_stored"], 16)

            run_steps(sp, step)
            sp.wait_ge(S["out_stored"], 16 * NT)

        @block.scalar
        def _(act):
            def sums(w, parts):
                for q in parts:
                    act.wait_ge(S[f"{w}_loaded{q}"], 16)
                    n = 4 * (w == "out") + q
                    if w == "out":
                        act.wait_ge(*(S["wo_abs"], 1) if q == 0 else (S["out_abs"], (2, 3, 1).index(q) + 1))
                    else:
                        act.wait_ge(*(S["qkv_abs"], 3) if q == 0 else (S["syn_abs"], q))
                    nc.scalar.activation(signs_b, (out_in if w == "out" else syn_in)[q], ACT.Abs,
                                         accum_out=pc[:, n:n + 1]).then_inc(S[f"{w}_abs"], 1)

            def sign(w, src, dst, thr):
                act.wait_ge(S[f"{w}_thr"], 1)
                nc.scalar.activation(dst, src, ACT.Sign, bias=thr, scale=BELOW).then_inc(S[f"{w}_sign"], 1)

            def qkv_sums(m):
                act.wait_ge(S[f"qkv_loaded{m}"], 16)
                if m:
                    act.wait_ge(S["qkv_abs"], m)
                nc.scalar.activation(signs_b, qkv_in[:, m].rearrange("p b d -> p (b d)"), ACT.Abs,
                                     accum_out=pc[:, 24 + m:25 + m]).then_inc(S["qkv_abs"], 1)

            def qkv_high(m):
                act.wait_ge(S["qkv_scale"], m + 1)
                nc.scalar.activation(wqkv[:, 0, :, m * E:(m + 1) * E], qkv_in[:, m], ACT.Copy,
                                     scale=pc[:, 36 + m:37 + m]).then_inc(S["qkv_whi"], 1)

            def step(act, i, p):
                a, b, t, u, d = (stage(i, p, k) for k in (2, 1, 0, -1, -2))
                tile0 = t and t.known and t.n == 0

                def qkv_out(b, m):
                    wait(act, "qkv_done", b, 3, m + 1)
                    if m == 0:
                        wait(act, "kv_done", b, 1, -1)
                        wait(act, "vd_ready", b, 1, -1)
                    dst = qk[:, b.par, m * E:(m + 1) * E] if m < 2 else v[:, b.par, :]
                    nc.scalar.activation(dst, proj[(b.par + m) % 2], ACT.Copy,
                                         scale=QS / (WS * XS)).then_inc(S["qkv_out"], 1)

                def heads_state():
                    wait(act, "state_ready", t, 1, 0)
                    if tile0:
                        act.wait_ge(S["constants"], 5)
                    for j in range(4):
                        head = slice(DH * j, DH * j + DH)
                        nc.scalar.activation(stateD[head, :, head], state[head, :].rearrange("p (g e) -> p g e", g=HG),
                                             ACT.Copy).then_inc(S["stateD_ready"], 1)

                if tile0:
                    heads_state()
                if t:
                    wait(act, "guess_ready", t, 1, 1)
                    wait(act, "z_out", t, 4, 4)
                    wait(act, "av_done", t, 4, 0)
                    if tile0:
                        act.wait_ge(S["synT3"], 16)
                    nc.scalar.activation(unused, z[:, t.par, :], ACT.Sign, bias=nt0, accum_out=s1).then_inc(S["sum1"], 1)
                if u:
                    wait(act, "h_ready", u, 1, 1)
                    wait(act, "hiT", u, 16, 0)
                    if u.known and u.n == 0:
                        act.wait_ge(S["outT2"], 16)
                    nc.scalar.activation(hl[:, 0, :], masked, ACT.Copy).then_inc(S["hi_ready"], 1)
                if b and not (b.known and b.n < 3):
                    qkv_out(b, 0)
                if t:
                    if not tile0:
                        heads_state()
                    wait(act, "nt_step", t, 5, 2)
                    nc.scalar.activation(unused, z[:, t.par, :], ACT.Sign, bias=nt1, accum_out=s2).then_inc(S["sum2"], 1)
                if u:
                    wait(act, "an_ready", u, 1, 1)
                    wait(act, "wo_done", u, 1, 0)
                    nc.scalar.activation(ahl[:, 0], aT, ACT.Copy).then_inc(S["ah_ready"], 1)
                if a:
                    wait(act, "xn_ready", a, 1, 1)
                    wait(act, "xT_ready", a, 16, 0)
                    nc.scalar.activation(xhl[:, 0, :], slot(xn, a), ACT.Copy).then_inc(S["xh_ready"], 1)
                    if a.known and a.n == 0:
                        qkv_sums(0)
                        qkv_sums(1)
                        qkv_high(0)
                        qkv_sums(2)
                        qkv_high(1)
                        qkv_high(2)
                if b and b.known and b.n == 0:
                    sums("syn", (0, 1))
                    qkv_out(b, 0)
                if t:
                    wait(act, "nt_step", t, 5, 5)
                    nc.scalar.activation(unused, z[:, t.par, :], ACT.Sign, bias=nt2, scale=BELOW,
                                         accum_out=s3).then_inc(S["sum3"], 1)
                if b and b.known and b.n == 0:
                    sums("syn", (2,))
                    qkv_out(b, 1)
                    sums("syn", (3,))
                    qkv_out(b, 2)
                    sign("syn", syn_in[1], signs_b, syn_thr[1])
                    sign("syn", syn_in[1], syn_t[1], syn_thr[0])
                    qkv_out(Tile(0, 1), 0)
                    wait(act, "rot_step", b, 4, 4)
                    sign("syn", syn_in[3], signs_c, syn_thr[1])
                    qkv_out(Tile(0, 1), 1)
                    sign("syn", syn_in[3], syn_t[3], syn_thr[0])
                    qkv_out(Tile(0, 1), 2)
                elif tile0:
                    sums("out", (2, 3, 1))
                elif b:
                    if not (b.known and b.n == 2):
                        qkv_out(b, 1)
                    qkv_out(b, 2)
                if t and t.known and t.n == 1:
                    act.wait_ge(S["out_loaded0"], 32)
                    act.wait_ge(S["out_tern"], 3)
                    sign("out", out_in[0], signs_b, out_thr[1])
                    act.wait_ge(S["al_ready"], 1)
                    sign("out", out_in[0], out_t[0], out_thr[0])
                if d:
                    wait(act, "yst", d, 5, 5)
                    nc.scalar.activation(y, y, ACT.Identity, scale=rD, bias=mrD).then_inc(S["yn_ready"], 1)
                if t:
                    wait(act, "av_done", t, 4, 4)
                    if t.known and t.n == 1:
                        act.wait_ge(S["outT0"], 16)
                    wait(act, "al_ready", t, 1, 0)
                    nc.scalar.activation(aT.rearrange("p g c -> p (g c)"), p_av, ACT.Copy).then_inc(S["aT_ready"], 1)
                    wait(act, "rall_done", t, 1, 0)
                    nc.scalar.activation(sq.rearrange("p g c -> p (g c)"), p_av, ACT.Square).then_inc(S["sq_ready"], 1)
                if b:
                    for m in range(2):
                        wait(act, "rot_step", b, 4, 4)
                        wait(act, "kST" if m else "qST", b, 16, 0)
                        src = qk[:, b.par, m * E:(m + 1) * E].rearrange("p (h d) -> p h d", h=H)
                        nc.scalar.activation(qks[:, m, :, 0:2 + m:1 + m, :], src.unsqueeze(2).to_broadcast([P, H, 2, DH]),
                                             ACT.Copy).then_inc(S["qk_hi"], 1)
                    if b.known and b.n == 0:
                        act.wait_ge(S["wo_scaled"], 1)
                        act.wait_ge(S["syn_tern"], 2)
                        nc.scalar.activation(signs_b, wo_in.rearrange("p b n -> p (b n)"), ACT.Abs,
                                             accum_out=pc[:, 60:61]).then_inc(S["wo_abs"], 1)
                        sums("out", (0,))
                        act.wait_ge(S["wo_scale"], 1)
                        nc.scalar.activation(wo[:, 0], wo_in, ACT.Copy, scale=pc[:, 63:64]).then_inc(S["wo_hi"], 1)
                if tile0:
                    sign("out", out_in[2], signs_b, out_thr[1])
                    act.wait_ge(S["synT0"], 16)
                    sign("out", out_in[2], out_t[2], out_thr[0])
                    qkv_out(Tile(1, 0), 0)
                    act.wait_ge(S["out_tern"], 1)
                    sign("out", out_in[1], signs_b, out_thr[1])
                    qkv_out(Tile(1, 0), 1)
                    act.wait_ge(S["synT1"], 16)
                    sign("out", out_in[1], out_t[1], out_thr[0])

            run_steps(act, step)

        @block.gpsimd
        def _(pool):
            nc.gpsimd.memset(mhalf, -0.5).then_inc(S["constants"], 1)
            nc.gpsimd.memset(half, 0.5).then_inc(S["constants"], 1)
            nc.gpsimd.memset(ones, 1.0).then_inc(S["constants"], 1)
            nc.gpsimd.memset(state, 0.0).then_inc(S["constants"], 1)
            nc.gpsimd.memset(stateD.rearrange("p g c -> p (g c)"), 0.0).then_inc(S["constants"], 1)
            pool.wait_ge(S["constants"], 5)

            def across(dst, src, op, name):
                nc.gpsimd.partition_all_reduce(dst, src, P, op).then_inc(S[name], 1)

            def step(pool, i, p):
                a, b, t, u, d = (stage(i, p, k) for k in (2, 1, 0, -1, -2))
                if u:
                    wait(pool, "veR_ready", u, 1, 1)
                    nc.gpsimd.tensor_tensor(rstdR, veR, mhalf, ALU.pow).then_inc(S["rstdR_ready"], 1)
                if t:
                    wait(pool, "qkv_out", t, 3, 3)
                    wait(pool, "kv_done", t, 1, 0)
                    if t.known and t.n == 0:
                        pool.wait_ge(S["tables_loaded"], 6 * 16)
                        pool.wait_ge(S["syn_tern"], 4)
                    nc.gpsimd.tensor_tensor(vd.rearrange("p (h e) -> p h e", h=H),
                                            v[:, t.par, :].rearrange("p (h e) -> p h e", h=H),
                                            kdec.unsqueeze(2).to_broadcast([P, H, DH]), ALU.mult).then_inc(S["vd_ready"], 1)
                if t:
                    wait(pool, "state_ready", t, 1, 0)
                    apart(pool)
                    ch = t.n % CHUNKS
                    k = rc[:, ch, :] if t.known else rc[:, bass.ds(ch, 1), :].rearrange("p a g -> p (a g)")
                    nc.gpsimd.tensor_tensor(kvs.rearrange("p (g e) -> p g e", g=HG), state.rearrange("p (g e) -> p g e", g=HG),
                                            k.unsqueeze(2).to_broadcast([P, HG, DH]), ALU.mult).then_inc(S["kvs_ready"], 1)
                if a:
                    wait(pool, "ln_stat", a, 3, 3)
                    nc.gpsimd.tensor_tensor(rstd, ve, mhalf, ALU.pow).then_inc(S["rstd_ready"], 1)
                    if a.known and a.n == 1:
                        for m in range(3):
                            pool.wait_ge(S["qkv_abs"], m + 1)
                            across(pc[:, 27 + m:28 + m], pc[:, 24 + m:25 + m], PMAX, "qkv_max")
                        pool.wait_ge(S["bsyn_max"], 1)
                        across(pc[:, 41:42], pc[:, 40:41], PMAX, "bsyn_all")
                if u and not (u.known and u.n >= NT - 2):
                    wait(pool, "hi_ready", u, 1, 1)
                    wait(pool, "loT", u, 16, 0)
                    if u.known and u.n == 0:
                        pool.wait_ge(S["outT1"], 16)
                    nc.gpsimd.tensor_tensor(hl[:, 1, :], masked, hl[:, 0, :], ALU.subtract).then_inc(S["lo_ready"], 1)
                if u and not (u.known and u.n == 0):
                    wait(pool, "ah_ready", u, 1, 1)
                    wait(pool, "wo_done", u, 1, 0)
                    nc.gpsimd.tensor_tensor(ahl[:, 1], aT, ahl[:, 0], ALU.subtract).then_inc(S["al_ready"], 1)
                if a:
                    wait(pool, "xh_ready", a, 1, 1)
                    apart(pool)
                    nc.gpsimd.tensor_tensor(xhl[:, 1, :], slot(xn, a), xhl[:, 0, :], ALU.subtract).then_inc(S["xl_ready"], 1)
                if d:
                    wait(pool, "yst", d, 5, 3)
                    nc.gpsimd.tensor_tensor(rstdD, veD, mhalf, ALU.pow).then_inc(S["rstdD_ready"], 1)
                if a:
                    def biases(a):
                        wait(pool, "xl_ready", a, 1, 1)
                        apart(pool)
                        nc.gpsimd.tensor_tensor(slot(xn, a), slot(xn, a), boutx, ALU.add).then_inc(S["xnb_ready"], 1)
                        apart(pool)
                        nc.gpsimd.tensor_tensor(slot(xr, a), slot(xr, a), bet, ALU.add).then_inc(S["beta_added"], 1)

                    if a.known and a.n == 1:
                        pool.wait_ge(S["qkv_wlo"], 3)
                        nc.gpsimd.memset(qks[:, :, :, 3, :], 0.0).then_inc(S["stack_zero"], 1)
                        pool.wait_ge(S["bout_ready"], 1)
                        biases(Tile(0, 0))
                    if not (a.known and a.n == 0):
                        biases(a)
                if b:
                    if b.known and b.n == 0:
                        pool.wait_ge(S["syn_rows"], 1)
                        across(pc[:, 17:18], pc[:, 16:17], PADD, "syn_sum")
                        pool.wait_ge(S["rot_loaded"], 16)
                    wait(pool, "qkv_out", b, 3, 2)
                    wait(pool, "inter_done", b, 1, 0)
                    ch = b.n % CHUNKS
                    trig = (rot[:, bass.ds(ch, 1)].rearrange("p a f e -> p (a f) e") if not b.known else rot[:, ch])
                    q4 = qk[:, b.par, :].rearrange("p (h a e) -> p h a e", a=2, e=16)
                    r4 = rt.rearrange("p (h a e) -> p h a e", a=2, e=8)
                    cos = trig[:, 0, :].unsqueeze(1).unsqueeze(1).to_broadcast([P, 2 * H, 2, 8])
                    for a_ in range(2):
                        sn = trig[:, 1 + a_, :].unsqueeze(1).to_broadcast([P, 2 * H, 8])
                        apart(pool)
                        nc.gpsimd.tensor_tensor(r4[:, :, a_], q4[:, :, 1 - a_, 0:8], sn,
                                                ALU.mult).then_inc(S["rot_step"], 1)
                    wait(pool, "rot_step", b, 4, 2)
                    apart(pool)
                    nc.gpsimd.tensor_tensor(q4[:, :, :, 0:8], q4[:, :, :, 0:8], cos, ALU.mult).then_inc(S["rot_step"], 1)
                    wait(pool, "rot_step", b, 4, 3)
                    nc.gpsimd.tensor_tensor(q4[:, :, :, 0:8], q4[:, :, :, 0:8], r4, ALU.add).then_inc(S["rot_step"], 1)
                    if b.known and b.n == 1:
                        pool.wait_ge(S["out_rows"], 1)
                        across(pc[:, 19:20], pc[:, 18:19], PADD, "out_sum")
                if d:
                    wait(pool, "yn_ready", d, 1, 1)
                    nc.gpsimd.tensor_tensor(y, y, gam, ALU.mult).then_inc(S["yg_ready"], 1)
                if t:
                    wait(pool, "sq_ready", t, 1, 1)
                    nc.gpsimd.tensor_tensor(sq[:, 0:2, :], sq[:, 0:2, :], sq[:, 2:4, :], ALU.add).then_inc(S["sq_sum"], 1)
                    wait(pool, "sq_sum", t, 2, 1)
                    nc.gpsimd.tensor_tensor(sq[:, 0, :], sq[:, 0, :], sq[:, 1, :], ALU.add).then_inc(S["sq_sum"], 1)
                if d:
                    wait(pool, "yg_ready", d, 1, 1)
                    apart(pool)
                    wait(pool, "att_added", d, 1, 1)
                    apart(pool)
                    wait(pool, "out_stored", d, 16, 0)
                    apart(pool)
                    nc.gpsimd.tensor_tensor(o, y, slot(xr, d), ALU.add).then_inc(S["out_ready"], 1)
                if b:
                    for m in range(2):
                        wait(pool, "qk_hi", b, 2, m + 1)
                        nc.gpsimd.tensor_tensor(qks[:, m, :, 2 - m, :],
                                                qk[:, b.par, m * E:(m + 1) * E].rearrange("p (h d) -> p h d", h=H),
                                                qks[:, m, :, 0, :], ALU.subtract).then_inc(S["qk_lo"], 1)
                    if b.known and b.n == 0:
                        pool.wait_ge(S["wo_abs"], 1)
                        across(pc[:, 61:62], pc[:, 60:61], PMAX, "wo_max")
                        pool.wait_ge(S["spread"], 1)
                        nc.gpsimd.tensor_tensor(pc[:, 55:56], pc[:, 52:53], half, ALU.pow).then_inc(S["spread_root"], 1)
                if t:
                    wait(pool, "fail_ready", t, 1, 1)
                    apart(pool)
                    nc.gpsimd.partition_all_reduce(failint, fail, P, PMAX).then_inc(S["fail_all"], 1)

            run_steps(pool, step)

        @block.tensor
        def _(pe):
            after = {(1, 0): ("qkv_out", 2), (1, 1): ("qkv_out", 3), (0, 3): ("qkv_out", 6), (0, 4): ("qkv_out", 5),
                     (1, 3): ("z_out", 4), (1, 4): ("z_out", 3)}

            def step(pe, i, p):
                b, t, u, d = (stage(i, p, k) for k in (1, 0, -1, -2))

                def projection(b, n):
                    wait(pe, "xT_ready", b, 16, 16)
                    if b.known and b.n < 2 and (b.n, n) in after:
                        pe.wait_ge(S[after[b.n, n][0]], after[b.n, n][1])
                    elif n < 2:
                        wait(pe, "z_out", b, 4, n - 1)
                    elif n < 5:
                        wait(pe, "qkv_out", b, 3, n - 1)
                    else:
                        wait(pe, "z_out", b, 4, n - 4)
                    if b.known and b.n == 0:
                        if n < 3:
                            pe.wait_ge(S["qkv_wlo"], n + 1)
                        else:
                            pe.wait_ge(S[f"synT{n - 3}"], 16)
                    if n < 3:
                        pairs = [(k + KB * l, wqkv[:, w, k, n * E:(n + 1) * E]) for k in range(KB)
                                 for l, w in ((0, 0), (0, 1), (1, 0))]
                    else:
                        pairs = [(k, wsynT[:, 4 * (n - 3):4 * (n - 2), k % KB, :]) for k in range(2 * KB)]
                    bank = proj[(b.par + n) % 2]
                    for m, (k, w) in enumerate(pairs):
                        last = nc.tensor.matmul(bank, xT[:, b.par, k, :], w, start=m == 0, stop=m == len(pairs) - 1)
                    last.then_inc(S["qkv_done" if n < 3 else "z_done"], 1)

                def scores(g):
                    if g == 0:
                        wait(pe, "qST", t, 16, 16)
                        wait(pe, "kST", t, 16, 16)
                        wait(pe, "P_ready", t, 4, 0)
                    elif g == 1:
                        wait(pe, "state_ready", t, 1, 0)
                    elif g == 2:
                        wait(pe, "qTd_ready", t, 1, 1)
                    else:
                        wait(pe, "P_ready", t, 4, 1)
                    for j in range(4):
                        h = 4 * g + j
                        last = nc.tensor.matmul(sbank[SCORES[g]][:, j * P:(j + 1) * P], qkst[0:96, 1, h, :],
                                                qkst[0:96, 0, h, :], start=True, stop=True)
                    last.then_inc(S["scores_done"], 1)

                def values(g):
                    wait(pe, "P_ready", t, 4, g + 1)
                    for j in range(4):
                        h = 4 * g + j
                        last = nc.tensor.matmul(p_av[32 * j:32 * j + 32, g * P:(g + 1) * P],
                                                v[:, t.par, h * DH:(h + 1) * DH], Pr[:, g % 2, j, :],
                                                start=False, stop=g == HG - 1, skip_group_check=True)
                    last.then_inc(S["av_done"], 1)

                def network(d):
                    wait(pe, "hiT", d, 16, 16)
                    wait(pe, "y_ready", d, 1, 0)
                    if d.known and d.n == 0:
                        for q in range(4):
                            pe.wait_ge(S[f"outT{q}"], 16)
                    for k in range(2 * NB):
                        if k == NB:
                            wait(pe, "loT", d, 16, 16)
                        last = nc.tensor.matmul(p_ffn, hT[:, k, :], woutT[:, k % NB, :], start=k == 0,
                                                stop=k == 2 * NB - 1)
                    last.then_inc(S["ffn_done"], 1)

                if d and not (d.known and d.n >= NT - 2):
                    network(d)
                def q_transposed():
                    wait(pe, "rot_step", t, 4, 4)
                    if t.known and t.n == 0:
                        pe.wait_ge(S["tables_loaded"], 6 * 16)
                        pe.wait_ge(S["constants"], 5)
                    wait(pe, "veR_ready", t, 1, 0)
                    for g in range(HG):
                        last = nc.tensor.transpose(sbank[0][:, g * P:(g + 1) * P],
                                                   qk[:, t.par, g * P:(g + 1) * P], ident)
                    last.then_inc(S["qT_done"], 1)
                if t and not (t.known and t.n == 1):
                    q_transposed()
                qkv = b and not (b.known and b.n == 1)
                if qkv:
                    projection(b, 0)
                def factors():
                    wait(pe, "rdiag_ready", u, 1, 1)
                    wait(pe, "att_added", u, 1, 0)
                    nc.tensor.matmul(p_wo[:, 0:P], ones, rdiag, start=True, stop=True).then_inc(S["rall_done"], 1)
                if u and not (u.known and u.n == 0):
                    factors()
                if qkv:
                    projection(b, 1)
                if qkv:
                    projection(b, 2)
                if t and t.known and t.n == 1:
                    q_transposed()
                if u and u.known and u.n == 0:
                    factors()
                if b and b.known and b.n == 0:
                    for n in range(3):
                        projection(Tile(0, 1), n)
                if t:
                    wait(pe, "qTd_ready", t, 1, 1)
                    wait(pe, "stateD_ready", t, 4, 4)
                    wait(pe, "sq_ready", t, 1, 0)
                    for g in range(HG):
                        last = nc.tensor.matmul(p_av[:, g * P:(g + 1) * P], stateD[:, g, :], qTd[:, g, :],
                                                start=g == 0, stop=False, skip_group_check=True)
                    last.then_inc(S["inter_done"], 1)
                    scores(0)
                    scores(1)
                    scores(2)
                if u and u.known and u.n == NT - 1:
                    network(u)
                if u:
                    wait(pe, "ah_ready", u, 1, 1)
                    wait(pe, "al_ready", u, 1, 1)
                    wait(pe, "att_added", u, 1, 0)
                    if u.known and u.n == 0:
                        pe.wait_ge(S["wo_ready"], 1)
                    pairs = [(l, w, g) for g in range(HG) for l, w in ((0, 0), (0, 1), (1, 0))]
                    for m, (l, w, g) in enumerate(pairs):
                        last = nc.tensor.matmul(p_wo, ahl[:, l, g, :], wo[:, w, g, :], start=m == 0, stop=m == len(pairs) - 1)
                    last.then_inc(S["wo_done"], 1)
                if b:
                    projection(b, 3)
                if t:
                    scores(3)
                    values(0)
                    values(1)
                if b:
                    projection(b, 4)
                if t:
                    values(2)
                    values(3)
                if b:
                    projection(b, 5)
                if t:
                    wait(pe, "vd_ready", t, 1, 1)
                    wait(pe, "P_ready", t, 4, 2)
                    apart(pe)
                    for h in range(H):
                        g, j = h // 4, h % 4
                        last = nc.tensor.matmul(sbank[2][32 * j:32 * j + 32, g * DH:(g + 1) * DH],
                                                qk[:, t.par, E + h * DH:E + (h + 1) * DH],
                                                vd[:, h * DH:(h + 1) * DH], start=True, stop=True)
                    last.then_inc(S["kv_done"], 1)
                if b:
                    projection(b, 6)
                if t:
                    wait(pe, "sq_sum", t, 2, 2)
                    wait(pe, "P_ready", t, 4, 3)
                    nc.tensor.matmul(sbank[0][:, 0:1], sq[:, 0, :], ones[:, 0:1], start=True, stop=True).then_inc(S["ss_done"], 1)
                    if t.known and t.n == NT - 1:
                        network(Tile(NT // 2 - 1, 0))

            run_steps(pe, step)

        @block.vector
        def _(dve):
            done = [0]

            def then(ins):
                done[0] += 1
                ins.then_inc(S["seed"], 1)
                dve.wait_ge(S["seed"], done[0])

            def pow2(dst, src):
                then(nc.vector.tensor_scalar(dst.bitcast(I32), src.bitcast(I32), 0x7F800000, None, ALU.bitwise_and))

            def ternary(w, src, dst, scratch, thr):
                then(nc.vector.tensor_scalar(scratch, src, thr[0], 2.0, ALU.is_gt, ALU.mult))
                then(nc.vector.tensor_scalar(dst, src, thr[1], 2.0, ALU.is_lt, ALU.mult))
                nc.vector.tensor_tensor(dst, scratch, dst, ALU.subtract).then_inc(S[f"{w}_tern"], 1)

            def ternary_of_signs(w, dst, other, n):
                dve.wait_ge(S[f"{w}_sign"], n)
                nc.vector.tensor_tensor(dst, dst, other, ALU.add).then_inc(S[f"{w}_tern"], 1)

            def factor(bound, power, scale, name):
                then(nc.vector.tensor_scalar(bound, bound, 1e-30, None, ALU.max))
                pow2(power, bound)
                then(nc.vector.reciprocal(scale, power))
                nc.vector.tensor_scalar(scale, scale, WS, None, ALU.mult).then_inc(S[name], 1)

            def qkv_weights():
                for m in range(3):
                    dve.wait_ge(S["qkv_max"], m + 1)
                    factor(pc[:, 27 + m:28 + m], pc[:, 33 + m:34 + m], pc[:, 36 + m:37 + m], "qkv_scale")
                    if m:
                        qkv_low(m - 1)
                    if m == 1:
                        biases()
                qkv_low(2)
                then(nc.vector.tensor_tensor(ppp, pc[:, 33:34], pc[:, 34:35], ALU.mult))
                then(nc.vector.tensor_tensor(ppp, ppp, pc[:, 35:36], ALU.mult))
                then(nc.vector.tensor_scalar(ppp, ppp, QS ** -3, None, ALU.mult))

            def qkv_low(m):
                dve.wait_ge(S["qkv_whi"], m + 1)
                dve.wait_ge(S["qkv_scale"], m + 1)
                nc.vector.scalar_tensor_tensor(wqkv[:, 1, :, m * E:(m + 1) * E], qkv_in[:, m], pc[:, 36 + m:37 + m],
                                               wqkv[:, 0, :, m * E:(m + 1) * E], ALU.mult,
                                               ALU.subtract).then_inc(S["qkv_wlo"], 1)

            def biases():
                dve.wait_ge(S["b_loaded"], 3 * 16)
                nc.vector.tensor_scalar(boutx, boutx, XS, None, ALU.mult).then_inc(S["bout_ready"], 1)
                then(nc.vector.tensor_reduce(pc[:, 40:41], bs16, AX.X, ALU.max))
                then(nc.vector.tensor_reduce(pc[:, 42:43], bs16, AX.X, ALU.min))
                then(nc.vector.tensor_scalar(pc[:, 42:43], pc[:, 42:43], -1.0, None, ALU.mult))
                nc.vector.tensor_tensor(pc[:, 40:41], pc[:, 40:41], pc[:, 42:43], ALU.max).then_inc(S["bsyn_max"], 1)

            def mean_abs(w, c0, c1, scale, thr):
                dve.wait_ge(S[f"{w}_abs"], 4)
                nc.vector.reduce_sum(pc[:, c1:c1 + 1], pc[:, c0:c0 + 4], AX.X).then_inc(S[f"{w}_rows"], 1)
                dve.wait_ge(S[f"{w}_sum"], 1)
                then(nc.vector.tensor_scalar(scale, pc[:, c1 + 1:c1 + 2], 1.0 / (N * E), None, ALU.mult))
                then(nc.vector.tensor_scalar(thr[0], scale, 1e-8, 0.5, ALU.add, ALU.mult))
                nc.vector.tensor_scalar(thr[1], thr[0], -1.0, None, ALU.mult).then_inc(S[f"{w}_thr"], 1)
                dve.wait_ge(S[f"{w}_thr"], 1)

            def syn_weights():
                mean_abs("syn", 0, 16, scale_syn, syn_thr)
                ternary("syn", syn_in[0], syn_t[0], signs_a, syn_thr)
                dve.wait_ge(S["rows_loaded"], 2 * 16)
                dve.wait_ge(S["bsyn_all"], 1)
                then(nc.vector.scalar_tensor_tensor(pc[:, 42:43], scale_syn, float(E), pc[:, 41:42], ALU.mult, ALU.add))
                then(nc.vector.tensor_scalar(pc[:, 42:43], pc[:, 42:43], 1e-30, None, ALU.max))
                pow2(pc[:, 43:44], pc[:, 42:43])
                then(nc.vector.reciprocal(pc[:, 44:45], pc[:, 43:44]))
                then(nc.vector.tensor_scalar(pc[:, 44:45], pc[:, 44:45], 16384.0, None, ALU.mult))
                then(nc.vector.scalar_tensor_tensor(gs, scale_syn, 0.5 / XS, pc[:, 44:45], ALU.mult, ALU.mult))
                ternary_of_signs("syn", syn_t[1], signs_b, 2)
                then(nc.vector.tensor_scalar(gb, gb, pc[:, 44:45], None, ALU.mult))
                ternary("syn", syn_in[2], syn_t[2], signs_a, syn_thr)
                ternary_of_signs("syn", syn_t[3], signs_c, 4)

            def step(dve, i, p):
                a, b, t, u, d = (stage(i, p, k) for k in (2, 1, 0, -1, -2))

                def probs(g):
                    wait(dve, "scores_done", t, 4, g + 1)
                    wait(dve, "av_done", t, 4, g - 1)
                    wait(dve, "sum3", t, 1, 1)
                    nc.vector.scalar_tensor_tensor(Pr[:, g % 2].rearrange("p j c -> p (j c)"), sbank[SCORES[g]], ppp,
                                                   dmask[:, 4 * g:4 * g + 4, :].rearrange("p j c -> p (j c)"),
                                                   ALU.mult, ALU.mult).then_inc(S["P_ready"], 1)

                def z_chunk(n):
                    wait(dve, "z_done", b, 4, n + 1)
                    if n == 0:
                        wait(dve, "h_ready", b, 1, -1)
                    nc.vector.scalar_tensor_tensor(z[:, b.par, n * 512:(n + 1) * 512], proj[(b.par + 3 + n) % 2], gs,
                                                   gb[:, n * 512:(n + 1) * 512], ALU.mult, ALU.add).then_inc(S["z_out"], 1)
                    if b.known and b.n == 0:
                        wait(dve, "z_out", b, 4, n + 1)
                        then(nc.vector.bn_stats(seed6[:, n, :], z[:, 0, n * 512:(n + 1) * 512]))
                        if n == 2:
                            dve.wait_ge(S["wo_max"], 1)
                            factor(pc[:, 61:62], pc[:, 62:63], pc[:, 63:64], "wo_scale")

                def attention_normed():
                    wait(dve, "rall_done", u, 1, 1)
                    wait(dve, "aT_ready", u, 1, 1)
                    nc.vector.scalar_tensor_tensor(aT, aT, AS, p_wo[:, 0:P].unsqueeze(1).to_broadcast([P, HG, P]), ALU.mult,
                                                   ALU.mult).then_inc(S["an_ready"], 1)

                def attention_added(u):
                    wait(dve, "wo_done", u, 1, 1)
                    wait(dve, "beta_added", u, 1, 1)
                    nc.vector.scalar_tensor_tensor(slot(xr, u), p_wo, wos, slot(xr, u), ALU.mult,
                                                   ALU.add).then_inc(S["att_added"], 1)

                def segments(k):
                    wait(dve, "w_out", t, 1, 1)
                    wait(dve, "top_step", t, 12, 0)
                    for n in range(4 * k, 4 * k + 4):
                        apart(dve)
                        nc.vector.max(cand[:, 0, 8 * n:8 * n + 8], masked[:, n * SEG:(n + 1) * SEG]).then_inc(S["seg_done"], 1)

                if u:
                    wait(dve, "kv_done", u, 1, 1)
                    wait(dve, "kvs_ready", u, 1, 1)
                    ch = u.n % CHUNKS
                    kp = keep[:, bass.ds(ch, 1)] if not u.known else keep[:, ch:ch + 1]
                    nc.vector.scalar_tensor_tensor(state, sbank[2][:, 0:P], kp, kvs, ALU.mult, ALU.add).then_inc(S["state_ready"], 1)
                    wait(dve, "ss_done", u, 1, 1)
                    nc.vector.tensor_scalar(veR, sbank[0][:, 0:1], 1.0 / E, LN_EPS, ALU.mult, ALU.add).then_inc(S["veR_ready"], 1)
                    wait(dve, "fail_all", u, 1, 1)
                    apart(dve)
                    missed = dve.value_load(failint[0:1, 0:1])
                    with dve.If(missed > 0):
                        wait(dve, "seg_done", u, 16, 16)
                        nc.vector.tensor_copy(masked, z[:, u.par, :]).then_inc(S["general"], 1)
                        with dve.Fori(0, TOPK // 8) as r:
                            dve.wait_ge(S["general"], u.n * FB + r * 2 + 1)
                            apart(dve)
                            nc.vector.max(fb8, masked).then_inc(S["general"], 1)
                            dve.wait_ge(S["general"], u.n * FB + r * 2 + 2)
                            apart(dve)
                            nc.vector.match_replace(masked, fb8, masked, -BIG).then_inc(S["general"], 1)
                        dve.wait_ge(S["general"], u.n * FB + FB - 2)
                        apart(dve)
                        nc.vector.max(fb8, masked).then_inc(S["general"], 1)
                        dve.wait_ge(S["general"], u.n * FB + FB - 1)
                        nc.vector.tensor_copy(val, fb8[:, TOPK % 8 - 1:TOPK % 8]).then_inc(S["general"], 1)
                    with dve.Else():
                        dve.sem_inc(S["general"], FB)
                    dve.wait_ge(S["general"], u.n * FB + FB)
                    nc.vector.tensor_scalar(thr, val, 0.0, None, ALU.max).then_inc(S["thr_ready"], 1)
                    nc.vector.tensor_scalar(vq, val, -0.25, None, ALU.mult).then_inc(S["guess_step"], 1)
                    wait(dve, "guess_step", u, 1, 1)
                    nc.vector.scalar_tensor_tensor(nt0, nt0, 0.75, vq, ALU.mult, ALU.add).then_inc(S["guess_ready"], 1)
                    wait(dve, "rstdR_ready", u, 1, 1)
                    nc.vector.tensor_scalar(rdiag, ident, rstdR, None, ALU.mult).then_inc(S["rdiag_ready"], 1)
                    if u.known and u.n == 0:
                        ternary_of_signs("out", out_t[1], signs_b, 4)
                    wait(dve, "thr_ready", u, 1, 1)
                    nc.vector.scalar_tensor_tensor(masked, z[:, u.par, :], thr, z[:, u.par, :], ALU.is_ge,
                                                   ALU.mult).then_inc(S["h_ready"], 1)
                if a:
                    dve.wait_ge(S[f"x_loaded{a.par}"], a.half * 16 + 16)
                    nc.vector.bn_stats(st6[:, 0, :], slot(xr, a)).then_inc(S["ln_stat"], 1)
                    wait(dve, "ln_stat", a, 3, 1)
                    apart(dve)
                    nc.vector.bn_aggr(mv, st6[:, 0:1, :]).then_inc(S["ln_stat"], 1)
                    wait(dve, "ln_stat", a, 3, 2)
                    nc.vector.tensor_scalar(ve, mv[:, 1:2], LN_EPS, None, ALU.add).then_inc(S["ln_stat"], 1)
                def q_decayed():
                    wait(dve, "qT_done", t, 1, 1)
                    nc.vector.scalar_tensor_tensor(qTd.rearrange("p g c -> p (g c)"), sbank[0], ppp,
                                                   qdec.rearrange("p g c -> p (g c)"), ALU.mult,
                                                   ALU.mult).then_inc(S["qTd_ready"], 1)

                if t and t.known and t.n == 0:
                    then(nc.vector.bn_aggr(pc[:, 50:52], seed6))
                    nc.vector.tensor_scalar(pc[:, 52:53], pc[:, 51:52], 1e-30, None, ALU.max).then_inc(S["spread"], 1)
                    dve.wait_ge(S["tables_loaded"], 6 * 16)
                    q_decayed()
                    dve.wait_ge(S["spread_root"], 1)
                    then(nc.vector.tensor_scalar(ndh, pc[:, 55:56], -0.5 / 359.4, None, ALU.mult))
                    then(nc.vector.tensor_scalar(off, pc[:, 55:56], 0.5 / 359.4 * (N - 2 * (TOPK - AIM)), None, ALU.mult))
                    then(nc.vector.tensor_scalar(pc[:, 56:57], pc[:, 50:51], -1.0, None, ALU.mult))
                    nc.vector.scalar_tensor_tensor(nt0, pc[:, 55:56], -1.2816, pc[:, 56:57], ALU.mult,
                                                   ALU.add).then_inc(S["guess_ready"], 1)
                    dve.wait_ge(S["wo_hi"], 1)
                    nc.vector.scalar_tensor_tensor(wo[:, 1], wo_in, pc[:, 63:64], wo[:, 0], ALU.mult,
                                                   ALU.subtract).then_inc(S["wo_ready"], 1)
                    then(nc.vector.tensor_scalar(wos, pc[:, 62:63], 1.0 / (WS * AS), None, ALU.mult))
                if t:
                    wait(dve, "guess_ready", t, 1, 1)
                    nc.vector.tensor_scalar(pre, nt0, off, None, ALU.subtract).then_inc(S["nt_step"], 1)
                    wait(dve, "sum1", t, 1, 1)
                    wait(dve, "nt_step", t, 5, 1)
                    nc.vector.tensor_scalar(nt1, s1, ndh, pre, ALU.mult, ALU.add).then_inc(S["nt_step"], 1)
                if a:
                    wait(dve, "rstd_ready", a, 1, 1)
                    nc.vector.tensor_scalar(r256, rstd, XS, None, ALU.mult).then_inc(S["r256_ready"], 1)
                    wait(dve, "r256_ready", a, 1, 1)
                    if a.known and a.n == 3:
                        dve.wait_ge(S["outT3"], 16)
                    nc.vector.tensor_scalar(slot(xn, a), slot(xr, a), mv[:, 0:1], r256, ALU.subtract,
                                            ALU.mult).then_inc(S["xn_ready"], 1)
                    if a.known and a.n == 1:
                        qkv_weights()
                if t:
                    if not (t.known and t.n == 0):
                        q_decayed()
                if u:
                    attention_normed()
                    if u.known and u.n >= NT - 2:
                        wait(dve, "hi_ready", u, 1, 1)
                        wait(dve, "loT", u, 16, 0)
                        nc.vector.tensor_tensor(hl[:, 1, :], masked, hl[:, 0, :], ALU.subtract).then_inc(S["lo_ready"], 1)
                if d:
                    wait(dve, "ffn_done", d, 1, 1)
                    wait(dve, "xnb_ready", d, 1, 1)
                    wait(dve, "out_ready", d, 1, 0)
                    if d.known and d.n == 0:
                        dve.wait_ge(S["out_tern"], 4)
                    nc.vector.scalar_tensor_tensor(y, p_ffn, so, slot(xn, d), ALU.mult, ALU.add).then_inc(S["y_ready"], 1)
                    wait(dve, "y_ready", d, 1, 1)
                    nc.vector.bn_stats(st6[:, 1, :], y).then_inc(S["yst"], 1)
                if t:
                    wait(dve, "nt_step", t, 5, 2)
                    nc.vector.tensor_scalar(pre, nt1, off, None, ALU.subtract).then_inc(S["nt_step"], 1)
                    wait(dve, "sum2", t, 1, 1)
                    wait(dve, "nt_step", t, 5, 3)
                    nc.vector.tensor_scalar(nt2, s2, ndh, pre, ALU.mult, ALU.add).then_inc(S["nt_step"], 1)
                    wait(dve, "nt_step", t, 5, 4)
                    nc.vector.tensor_scalar(t2, nt2, -1.0, None, ALU.mult).then_inc(S["nt_step"], 1)
                if d:
                    wait(dve, "yst", d, 5, 1)
                    apart(dve)
                    nc.vector.bn_aggr(mvD, st6[:, 1:2, :]).then_inc(S["yst"], 1)
                    wait(dve, "yst", d, 5, 2)
                    nc.vector.tensor_scalar(veD, mvD[:, 1:2], 1.0 / (XS * XS), LN_EPS, ALU.mult, ALU.add).then_inc(S["yst"], 1)

                if u and u.known and u.n == 0:
                    wait(dve, "ah_ready", u, 1, 1)
                    nc.vector.tensor_tensor(ahl[:, 1], aT, ahl[:, 0], ALU.subtract).then_inc(S["al_ready"], 1)

                def below():
                    wait(dve, "nt_step", t, 5, 5)
                    wait(dve, "lo_ready", t, 1, 0)
                    nc.vector.scalar_tensor_tensor(masked, z[:, t.par, :], t2, z[:, t.par, :], ALU.is_le,
                                                   ALU.mult).then_inc(S["w_out"], 1)

                tile0 = t and t.known and t.n == 0
                if t:
                    below()
                if d:
                    wait(dve, "rstdD_ready", d, 1, 1)
                    nc.vector.tensor_scalar(rD, rstdD, 1.0 / XS, None, ALU.mult).then_inc(S["yst"], 1)
                    wait(dve, "yst", d, 5, 4)
                    nc.vector.scalar_tensor_tensor(mrD, mvD[:, 0:1], -1.0, rD, ALU.mult, ALU.mult).then_inc(S["yst"], 1)
                if tile0:
                    dve.wait_ge(S["dmask_loaded"], 16)
                if t:
                    probs(0)
                    probs(1)
                    segments(0)
                    if t.known and t.n == 1:
                        ternary_of_signs("out", out_t[0], signs_b, 6)
                if b:
                    if b.known and b.n == 0:
                        syn_weights()
                        dve.wait_ge(S["wo_loaded"], 2 * 16)
                        for k in range(KB):
                            last = nc.vector.tensor_scalar(wo_in[:, k, :], wo_in[:, k, :], rmsw[:, k:k + 1], None, ALU.mult)
                        last.then_inc(S["wo_scaled"], 1)
                    z_chunk(0)
                if t:
                    probs(2)
                    probs(3)
                    segments(1)
                if b:
                    z_chunk(1)
                if u and not (u.known and u.n == NT - 1):
                    attention_added(u)
                if d and d.known and d.n == NT - 1:
                    attention_added(d)
                if tile0:
                    mean_abs("out", 4, 18, scale_out, out_thr)
                    then(nc.vector.scalar_tensor_tensor(so, scale_out, 0.5 * XS / 16384.0, pc[:, 43:44], ALU.mult,
                                                        ALU.mult))
                if t:
                    segments(2)
                if b:
                    z_chunk(2)
                if t:
                    segments(3)
                if tile0:
                    z_chunk(3)
                if t:
                    wait(dve, "sum3", t, 1, 1)
                    nc.vector.tensor_scalar(rank, s3, -0.5, TOPK - N / 2, ALU.mult, ALU.add).then_inc(S["top_step"], 1)
                    wait(dve, "seg_done", t, 16, 16)
                    nc.vector.tensor_reduce(m8, cand[:, 0, :].rearrange("p (s k) -> p s k", k=8)[:, :, 7], AX.X,
                                            ALU.max).then_inc(S["top_step"], 1)
                    for r in range(RANKS // 8):
                        apart(dve)
                        nc.vector.max(top[:, 8 * r:8 * r + 8], cand[:, r % 2, :]).then_inc(S["top_step"], 1)
                        if r < RANKS // 8 - 1:
                            wait(dve, "top_step", t, 12, 3 + 2 * r)
                            apart(dve)
                            nc.vector.match_replace(cand[:, (r + 1) % 2, :], top[:, 8 * r:8 * r + 8], cand[:, r % 2, :],
                                                    -BIG).then_inc(S["top_step"], 1)
                            wait(dve, "top_step", t, 12, 4 + 2 * r)
                    wait(dve, "top_step", t, 12, 9)
                    nc.vector.scalar_tensor_tensor(sel, iota, rank, top, ALU.is_equal, ALU.mult,
                                                   accum_out=val).then_inc(S["top_step"], 1)
                    wait(dve, "top_step", t, 12, 10)
                    nc.vector.tensor_scalar(pre, val, 0.0, None, ALU.is_le).then_inc(S["top_step"], 1)
                    nc.vector.tensor_tensor(s1, m8, val, ALU.is_gt).then_inc(S["top_step"], 1)
                    wait(dve, "top_step", t, 12, 12)
                    nc.vector.tensor_tensor(fail, pre, s1, ALU.max).then_inc(S["fail_ready"], 1)
                if b and not tile0:
                    z_chunk(3)

                if tile0:
                    ternary_of_signs("out", out_t[2], signs_b, 2)
                    wait(dve, "av_done", t, 4, 4)
                    ternary("out", out_in[3], out_t[3], unused, out_thr)

            run_steps(dve, step)


_INS = ["L0_attn_x", "L0_attn_Wq", "L0_attn_Wk", "L0_attn_Wv", "L0_attn_Wo", "L0_attn_rms_w", "L0_ffn_W_syn",
        "L0_ffn_b_syn", "L0_ffn_W_out", "L0_ffn_b_out", "L0_ffn_gamma", "L0_ffn_beta"]


def tables():
    import numpy as np

    f = np.float32
    freq = (f(1.0 / 1024.0) ** np.linspace(0.0, 1.0, DH // 4, dtype=f)).astype(f)
    theta = (np.arange(CHUNKS * P, dtype=f)[:, None] * freq[None, :]).astype(f).astype(np.float64)
    cos, sin = np.cos(theta), np.sin(theta)
    rot = np.stack([cos, sin, -sin], 1).reshape(CHUNKS, P, 3, 8).transpose(1, 0, 2, 3)
    start = 2.0 ** (-2.0 ** (-(np.log2(H) - 3)))
    slopes = np.array([start * start ** i for i in range(H)]).astype(f)
    r = np.exp(-slopes.astype(np.float64)).astype(f).astype(np.float64)
    i = np.arange(P)
    diff = i[None, :] - i[:, None]
    dmask = np.where(diff[:, None, :] >= 0, r[None, :, None] ** np.maximum(diff, 0)[:, None, :], 0.0)
    rg = r.reshape(HG, 4)
    qdec = np.repeat(rg.T, DH, axis=0)[:, :, None] ** (i[None, None, :] + 1.0)
    kdec = r[None, :] ** (127.0 - i[:, None])
    keep = np.tile((np.arange(CHUNKS) < CHUNKS - 1).astype(f), (P, 1))
    rc = keep[:, :, None] * np.repeat(rg.T ** 128.0, DH, axis=0)[:, None, :]
    iota = np.tile(np.arange(1, RANKS + 1, dtype=f), (P, 1))
    return {k: np.ascontiguousarray(a, dtype=f) for k, a in dict(
        t_rot=rot, t_dmask=dmask, t_qdec=qdec, t_kdec=kdec, t_rc=rc, t_keep=keep, t_ident=np.eye(P),
        t_iota=iota).items()}


def kernel(**inputs):
    import numpy as _np
    import concourse.bacc as _bacc
    from concourse import mybir as _mybir
    from concourse.bass_utils import run_bass_kernel_spmd as _run

    nc = _bacc.Bacc("TRN2", target_bir_lowering=False, num_devices=1)
    arrays, args = {}, []
    for name in _INS:
        a = _np.ascontiguousarray(inputs[name])
        if name == "L0_attn_x":
            a = a.reshape(NT * P, E)
        if name == "L0_attn_rms_w":
            a = _np.ascontiguousarray(a.reshape(KB, P).T)
        arrays[f"in_{name}_dram"] = a
        args.append(nc.dram_tensor(f"in_{name}_dram", a.shape, _mybir.dt.from_np(a.dtype), kind="ExternalInput").ap())
    for name, a in tables().items():
        arrays[f"{name}_dram"] = a
        args.append(nc.dram_tensor(f"{name}_dram", a.shape, _mybir.dt.from_np(a.dtype), kind="ExternalInput").ap())
    args.append(nc.dram_tensor("out_0_dram", (NT * P, E), F32, kind="ExternalOutput").ap())
    build(nc, *args)
    r = _run(nc, [arrays], core_ids=[0])
    return r.results[0]["out_0_dram"].reshape(4, NT * P // 4, E)
```
